# Optimizing a Trainium2 kernel written in Bass

```python
import numpy as np
import jax
import jax.numpy as jnp

def _softmax(x, axis=-1):
    return jax.nn.softmax(x, axis=axis)

def _gelu(x):
    return jax.nn.gelu(x, approximate=True)

def _silu(x):
    return jax.nn.silu(x)

def _sigmoid(x):
    return jax.nn.sigmoid(x)

def _layernorm(x, axis=-1, eps=1e-05):
    m = jnp.mean(x, axis=axis, keepdims=True)
    v = jnp.var(x, axis=axis, keepdims=True)
    return (x - m) / jnp.sqrt(v + eps)

def _scatter_add(tgt, idx, src, axis=0):
    return tgt.at[idx].add(src)

def _segment_sum(src, seg, n):
    return jax.ops.segment_sum(src, seg, n)
kernel_name = 'mk_gnn_ffn_d1_gnn_r8_45f413'

def setup_inputs(seed: int=0):
    np.random.seed(seed)
    _w = jnp.asarray

    def _rec_inputs():
        import jax
        import jax.numpy as jnp
        _gk = jax.random.key(seed)
        x = -8.776e-05 + 1 * jax.random.normal(jax.random.fold_in(_gk, 1), (6250, 256), jnp.float32)
        src = jax.random.randint(jax.random.fold_in(_gk, 2), (200000,), 0, 6250, jnp.int32)
        dst = jnp.minimum((6250 * jax.random.uniform(jax.random.fold_in(_gk, 3), (200000,)) ** 2.0).astype(jnp.int32), 49999)
        _o = jnp.argsort(dst, stable=True)
        src = src[_o]
        dst = dst[_o]
        return (x, src, dst)
    x, src, dst = _rec_inputs()

    def _L0_gnn_setup():
        import jax, jax.numpy as jnp
        import numpy as np
        N = 2500
        E = 40000
        HID = 256
        HEADS = 8
        HD = HID // HEADS
        key = jax.random.key(seed)
        ks = jax.random.split(key, 12)
        scale = 1.0 / np.sqrt(HID).astype(np.float32)

        def lin_w(k):
            return jax.random.normal(k, (HID, HID), jnp.float32) * scale

        def lin_b(k):
            return jax.random.normal(k, (HID,), jnp.float32) * 0.01
        return {'h': jax.random.normal(ks[0], (N, HID), jnp.float32), 'Wq': lin_w(ks[1]), 'bq': lin_b(ks[2]), 'Wk': lin_w(ks[3]), 'bk': lin_b(ks[4]), 'Wv': lin_w(ks[5]), 'bv': lin_b(ks[6]), 'Wo': lin_w(ks[7]), 'bo': lin_b(ks[8]), 'rows': jax.random.randint(ks[9], (E,), 0, N), 'cols': jax.random.randint(ks[10], (E,), 0, N)}
    _L0_gnn_all = _L0_gnn_setup()
    _L0_gnn_in = {k: v for k, v in _L0_gnn_all.items() if k in ('Wq', 'bq', 'Wk', 'bk', 'Wv', 'bv', 'Wo', 'bo')}
    del _L0_gnn_all

    def _L0_ffn_setup():
        import jax, jax.numpy as jnp
        import numpy as np
        B, N, D = (16, 512, 256)
        NUM_EXPERTS, TOP_K, HEADS = (4, 2, 4)
        N_EDGES = 131072
        LN_EPS = 1e-05

        def _layernorm(x, g, b):
            mu = x.mean(-1, keepdims=True)
            var = ((x - mu) ** 2).mean(-1, keepdims=True)
            return (x - mu) * jax.lax.rsqrt(var + LN_EPS) * g + b

        def _forward(x, edge_index, W_gat, att_src, att_dst, b_gat, ln_gamma, ln_beta, W1, b1, W2, b2):
            Bc, Nc, Dc = x.shape
            M = Bc * Nc
            x_flat = x.reshape(M, Dc)
            h = (x_flat @ W_gat).reshape(M, HEADS, NUM_EXPERTS)
            loops = jnp.arange(M, dtype=edge_index.dtype)
            src = jnp.concatenate([edge_index[0], loops])
            dst = jnp.concatenate([edge_index[1], loops])
            a_src = (h * att_src).sum(-1)
            a_dst = (h * att_dst).sum(-1)
            e = jax.nn.leaky_relu(a_src[src] + a_dst[dst], negative_slope=0.2)
            e_max = jax.ops.segment_max(e, dst, num_segments=M)
            ee = jnp.exp(e - e_max[dst])
            denom = jax.ops.segment_sum(ee, dst, num_segments=M)
            alpha = ee / (denom[dst] + 1e-16)
            msg = h[src] * alpha[:, :, None]
            agg = jax.ops.segment_sum(msg, dst, num_segments=M).reshape(M, HEADS * NUM_EXPERTS) + b_gat
            scores = _layernorm(agg, ln_gamma, ln_beta).reshape(M, HEADS, NUM_EXPERTS).mean(1)
            scores = scores.reshape(Bc, Nc, NUM_EXPERTS)
            topk_s, topk_i = jax.lax.top_k(scores, TOP_K)
            w = jax.nn.softmax(topk_s, axis=-1)
            out = jnp.zeros_like(x)
            for ei in range(NUM_EXPERTS):
                g = jnp.where(topk_i == ei, w, 0.0).sum(-1)
                hh = jax.nn.gelu(x @ W1[ei] + b1[ei], approximate=False)
                out = out + g[..., None] * (hh @ W2[ei] + b2[ei])
            return out
        key = jax.random.key(seed)
        ks = jax.random.split(key, 8)
        s = 0.05
        return {'x': jax.random.normal(ks[0], (B, N, D), jnp.float32), 'W_gat': jax.random.normal(ks[1], (D, HEADS * NUM_EXPERTS), jnp.float32) * s, 'att_src': jax.random.normal(ks[2], (HEADS, NUM_EXPERTS), jnp.float32) * s, 'att_dst': jax.random.normal(ks[3], (HEADS, NUM_EXPERTS), jnp.float32) * s, 'b_gat': jnp.zeros((HEADS * NUM_EXPERTS,), jnp.float32), 'ln_gamma': jnp.ones((HEADS * NUM_EXPERTS,), jnp.float32), 'ln_beta': jnp.zeros((HEADS * NUM_EXPERTS,), jnp.float32), 'W1': jax.random.normal(ks[4], (NUM_EXPERTS, D, 2 * D), jnp.float32) * s, 'b1': jnp.zeros((NUM_EXPERTS, 2 * D), jnp.float32), 'W2': jax.random.normal(ks[5], (NUM_EXPERTS, 2 * D, D), jnp.float32) * s, 'b2': jnp.zeros((NUM_EXPERTS, D), jnp.float32), 'edge_index': jax.random.randint(ks[6], (2, N_EDGES), 0, B * N, jnp.int32)}
    _L0_ffn_all = _L0_ffn_setup()
    _L0_ffn_in = {k: v for k, v in _L0_ffn_all.items() if k in ('W_gat', 'att_src', 'att_dst', 'b_gat', 'ln_gamma', 'ln_beta', 'W1', 'b1', 'W2', 'b2', 'edge_index')}
    del _L0_ffn_all
    return {'x': x, 'src': src, 'dst': dst, 'L0_gnn_Wq': _L0_gnn_in['Wq'], 'L0_gnn_bq': _L0_gnn_in['bq'], 'L0_gnn_Wk': _L0_gnn_in['Wk'], 'L0_gnn_bk': _L0_gnn_in['bk'], 'L0_gnn_Wv': _L0_gnn_in['Wv'], 'L0_gnn_bv': _L0_gnn_in['bv'], 'L0_gnn_Wo': _L0_gnn_in['Wo'], 'L0_gnn_bo': _L0_gnn_in['bo'], 'L0_ffn_W_gat': _L0_ffn_in['W_gat'], 'L0_ffn_att_src': _L0_ffn_in['att_src'], 'L0_ffn_att_dst': _L0_ffn_in['att_dst'], 'L0_ffn_b_gat': _L0_ffn_in['b_gat'], 'L0_ffn_ln_gamma': _L0_ffn_in['ln_gamma'], 'L0_ffn_ln_beta': _L0_ffn_in['ln_beta'], 'L0_ffn_W1': _L0_ffn_in['W1'], 'L0_ffn_b1': _L0_ffn_in['b1'], 'L0_ffn_W2': _L0_ffn_in['W2'], 'L0_ffn_b2': _L0_ffn_in['b2'], 'L0_ffn_edge_index': _L0_ffn_in['edge_index']}

def reference(x, src, dst, L0_gnn_Wq, L0_gnn_bq, L0_gnn_Wk, L0_gnn_bk, L0_gnn_Wv, L0_gnn_bv, L0_gnn_Wo, L0_gnn_bo, L0_ffn_W_gat, L0_ffn_att_src, L0_ffn_att_dst, L0_ffn_b_gat, L0_ffn_ln_gamma, L0_ffn_ln_beta, L0_ffn_W1, L0_ffn_b1, L0_ffn_W2, L0_ffn_b2, L0_ffn_edge_index):
    import jax
    import jax.numpy as jnp

    def _L0_gnn_ref(h, Wq, bq, Wk, bk, Wv, bv, Wo, bo, rows, cols):
        import jax, jax.numpy as jnp
        import numpy as np
        N = 2500
        E = 40000
        HID = 256
        HEADS = 8
        HD = HID // HEADS
        n = h.shape[0]
        scaling = HD ** (-0.5)
        q = (h @ Wq + bq).reshape(n, HD, HEADS) * scaling
        k = (h @ Wk + bk).reshape(n, HD, HEADS)
        v = (h @ Wv + bv).reshape(n, HD, HEADS)
        s = jnp.einsum('edh,edh->eh', q[rows], k[cols])
        m = jax.ops.segment_max(s, rows, num_segments=n)
        e = jnp.exp(s - m[rows])
        z = jax.ops.segment_sum(e, rows, num_segments=n)
        attn = e / z[rows]
        out = jax.ops.segment_sum(attn[:, None, :] * v[cols], rows, num_segments=n)
        return out.reshape(n, -1) @ Wo + bo

    def _L0_ffn_ref(x, W_gat, att_src, att_dst, b_gat, ln_gamma, ln_beta, W1, b1, W2, b2, edge_index):
        import jax, jax.numpy as jnp
        import numpy as np
        B, N, D = (16, 512, 256)
        NUM_EXPERTS, TOP_K, HEADS = (4, 2, 4)
        N_EDGES = 131072
        LN_EPS = 1e-05

        def _layernorm(x, g, b):
            mu = x.mean(-1, keepdims=True)
            var = ((x - mu) ** 2).mean(-1, keepdims=True)
            return (x - mu) * jax.lax.rsqrt(var + LN_EPS) * g + b

        def _forward(x, edge_index, W_gat, att_src, att_dst, b_gat, ln_gamma, ln_beta, W1, b1, W2, b2):
            Bc, Nc, Dc = x.shape
            M = Bc * Nc
            x_flat = x.reshape(M, Dc)
            h = (x_flat @ W_gat).reshape(M, HEADS, NUM_EXPERTS)
            loops = jnp.arange(M, dtype=edge_index.dtype)
            src = jnp.concatenate([edge_index[0], loops])
            dst = jnp.concatenate([edge_index[1], loops])
            a_src = (h * att_src).sum(-1)
            a_dst = (h * att_dst).sum(-1)
            e = jax.nn.leaky_relu(a_src[src] + a_dst[dst], negative_slope=0.2)
            e_max = jax.ops.segment_max(e, dst, num_segments=M)
            ee = jnp.exp(e - e_max[dst])
            denom = jax.ops.segment_sum(ee, dst, num_segments=M)
            alpha = ee / (denom[dst] + 1e-16)
            msg = h[src] * alpha[:, :, None]
            agg = jax.ops.segment_sum(msg, dst, num_segments=M).reshape(M, HEADS * NUM_EXPERTS) + b_gat
            scores = _layernorm(agg, ln_gamma, ln_beta).reshape(M, HEADS, NUM_EXPERTS).mean(1)
            scores = scores.reshape(Bc, Nc, NUM_EXPERTS)
            topk_s, topk_i = jax.lax.top_k(scores, TOP_K)
            w = jax.nn.softmax(topk_s, axis=-1)
            out = jnp.zeros_like(x)
            for ei in range(NUM_EXPERTS):
                g = jnp.where(topk_i == ei, w, 0.0).sum(-1)
                hh = jax.nn.gelu(x @ W1[ei] + b1[ei], approximate=False)
                out = out + g[..., None] * (hh @ W2[ei] + b2[ei])
            return out
        return _forward(x, edge_index, W_gat, att_src, att_dst, b_gat, ln_gamma, ln_beta, W1, b1, W2, b2)
    x = x + _L0_gnn_ref(_layernorm(x, axis=-1), L0_gnn_Wq, L0_gnn_bq, L0_gnn_Wk, L0_gnn_bk, L0_gnn_Wv, L0_gnn_bv, L0_gnn_Wo, L0_gnn_bo, src, dst)
    x = x + _L0_ffn_ref(_layernorm(x, axis=-1)[None], L0_ffn_W_gat, L0_ffn_att_src, L0_ffn_att_dst, L0_ffn_b_gat, L0_ffn_ln_gamma, L0_ffn_ln_beta, L0_ffn_W1, L0_ffn_b1, L0_ffn_W2, L0_ffn_b2, L0_ffn_edge_index)[0]
    return x

_drawn_inputs = setup_inputs


def setup_inputs(seed=0):
    import zlib

    import numpy as np

    out = dict(_drawn_inputs(seed))
    spreads = {'L0_ffn_b_gat': (0.0, 0.1),
     'L0_ffn_ln_gamma': (1.0, 0.2),
     'L0_ffn_ln_beta': (0.0, 0.1),
     'L0_ffn_b1': (0.0, 0.1),
     'L0_ffn_b2': (0.0, 0.1)}
    factors = {'L0_gnn_bq': 5.684, 'L0_gnn_bk': 8.0}
    for name, (base, spread) in spreads.items():
        noise = np.random.default_rng([zlib.crc32(name.encode()), seed]).standard_normal(out[name].shape)
        drawn = base * np.exp(spread * noise) if base else spread * noise
        out[name] = jnp.asarray(drawn.astype(out[name].dtype))
    for name, factor in factors.items():
        out[name] = (out[name] * factor).astype(out[name].dtype)
    return out
```

```python
from contextlib import ExitStack

import concourse.bass as bass
from concourse import mybir

F32 = mybir.dt.float32
BF16 = mybir.dt.bfloat16
I32 = mybir.dt.int32
ALU = mybir.AluOpType
ACT = mybir.ActivationFunctionType
AX = mybir.AxisListType

P = 128
N = 6250
D = 256
NB = 50
NPAD = NB * P
FULL = N // P
REST = N - FULL * P
EPS = 1e-5
LOWEST = -1.0e38

HEADS = 8
HD = D // HEADS
GH = 4
EX = 4
GROW = GH * EX + GH
FF = 512
U = 10

BLOCKS = 49
KEYS_HI = 64
FAR = float(1 << 20)
PAD_KEY = KEYS_HI * P - 1
SHIFT = 8
STEP = (1 << SHIFT) // P
HALF = 8


class Edges:

    def __init__(self, name, edges, tiles, chunks, chunk):
        self.name, self.tiles, self.chunks, self.chunk = name, tiles, chunks, chunk
        self.slots = chunks * chunk
        self.items = self.slots // STEP
        self.pos = self.slots * P
        assert tiles * P >= edges and tiles % (2 * HALF) == 0 and self.slots % STEP == 0
        assert (edges + BLOCKS * (STEP * P - 1)) // (STEP * P) <= self.items


ATT = Edges("att", 200000, 1568, 13, 128)
GAT = Edges("gat", 131072 + BLOCKS * P, 1088, 12, 98)


AI = 8
GI = 14


class Region:

    def __init__(self, nc, tag):
        self.nc, self.tag, self.ctx, self.sems = nc, tag, ExitStack(), []

    def __enter__(self):
        return self

    def __exit__(self, *e):
        if self.sems and e[0] is None:
            self.nc.clear_and_free_semaphores(self.sems)
            self.nc.all_engine_barrier()
        return self.ctx.__exit__(*e)

    def sb(self, name, shape, dt=F32):
        return self.ctx.enter_context(self.nc.sbuf_tensor(f"{self.tag}_{name}", shape, dt))

    def ps(self, name, shape, dt=F32):
        return self.ctx.enter_context(self.nc.psum_tensor(f"{self.tag}_{name}", shape, dt))

    def sem(self, name):
        self.sems.append(self.nc.alloc_semaphore(f"{self.tag}_{name}"))
        return self.sems[-1]


class Chain:

    def __init__(self, eng, sem, n=0):
        self.eng, self.sem, self.n = eng, sem, n

    def inc(self, instruction):
        instruction.then_inc(self.sem, 1)
        self.n += 1

    def wait(self):
        self.eng.wait_ge(self.sem, self.n)


def bc(ap, shape):
    return ap.to_broadcast(shape)


def constants(nc, c):
    with Region(nc, "const") as r:
        made = r.sem("const_made")
        iota_i = r.sb("iota_i", [P, P], I32)
        col_i = r.sb("col_i", [P, 1], I32)
        with nc.Block() as block:
            @block.gpsimd
            def _(e):
                e.memset(c["ident"][:], 0.0).then_inc(made, 1)
                e.iota(iota_i[:], pattern=[[1, P]], base=0, channel_multiplier=0).then_inc(made, 1)
                e.iota(col_i[:], pattern=[[1, 1]], base=0, channel_multiplier=1).then_inc(made, 1)
                e.wait_ge(made, 3)
                e.affine_select(out=c["ident"][:], in_=c["ident"][:], compare_op=ALU.not_equal, fill=1.0,
                                base=0, pattern=[[-1, P]], channel_multiplier=1).then_inc(made, 1)
                e.tensor_copy(c["iota"][:], iota_i[:]).then_inc(made, 1)
                e.tensor_copy(c["col"][:], col_i[:]).then_inc(made, 1)
                e.wait_ge(made, 6)


def normalise(nc, tag, x_sb, xc, rstd, load=None):
    with Region(nc, tag) as r:
        mean = r.sb("mean", [P, NB])
        sq = r.sb("sq", [P, NB // 5, D])
        x_loaded, stat, squared, root = r.sem("x_loaded"), r.sem("stat"), r.sem("squared"), r.sem("root")
        with nc.Block() as block:
            @block.sync
            def _(e):
                if load is not None:
                    e.wait_ge(stat, 1)
                    e.dma_start(x_sb[:, 0:FULL, :], load[0:FULL * P, :].rearrange("(b p) d -> p b d", p=P)).then_inc(x_loaded, 16)
                    e.dma_start(x_sb[0:REST, FULL, :], load[FULL * P:N, :]).then_inc(x_loaded, 16)
                    e.wait_ge(x_loaded, 32)

            @block.vector
            def _(v):
                ch = Chain(v, stat)
                if load is not None:
                    ch.inc(v.memset(x_sb[:, FULL:NB, :], 0.0))
                    v.wait_ge(x_loaded, 32)
                ch.inc(v.tensor_reduce(mean[:], x_sb[:], AX.X, ALU.add))
                ch.wait()
                ch.inc(v.tensor_scalar(mean[:], mean[:], 1.0 / D, None, ALU.mult))
                ch.wait()
                ch.inc(v.tensor_tensor(xc[:], x_sb[:], bc(mean[:].unsqueeze(2), [P, NB, D]), ALU.subtract))
                ch.wait()
                for b in range(0, NB, NB // 5):
                    half = slice(b, b + NB // 5)
                    ch.inc(v.tensor_tensor(sq[:], xc[:, half, :], xc[:, half, :], ALU.mult))
                    ch.wait()
                    ch.inc(v.tensor_reduce(rstd[:, half], sq[:], AX.X, ALU.add))
                    ch.wait()
                v.tensor_scalar(rstd[:], rstd[:], 1.0 / D, EPS, ALU.mult, ALU.add).then_inc(squared, 1)
                v.wait_ge(root, 1)
                ch.inc(v.reciprocal(rstd[:], rstd[:]))
                ch.wait()

            @block.scalar
            def _(a):
                a.wait_ge(squared, 1)
                a.activation(rstd[:], rstd[:], ACT.Sqrt).then_inc(root, 1)


def project(nc, c, xc, rstd, w, q_sb, kv):
    with Region(nc, "proj") as r:
        W = r.sb("W", [P, 2, 3 * D])
        brow = r.sb("brow", [P, 3 * D])
        stage = r.sb("stage", [P, 2, D])
        xT = r.sb("xT", [P, 2, D])
        rows = r.sb("rows", [P, 2, 2 * D])
        psT = [r.ps(f"psT{i}", [P, D]) for i in range(2)]
        psqk = [r.ps(f"psqk{i}", [P, 2 * D]) for i in range(2)]
        psv = [r.ps(f"psv{i}", [P, D]) for i in range(2)]
        w_loaded, w_ready = r.sem("w_loaded"), r.sem("w_ready")
        staged, turned, xT_ready = r.sem("staged"), r.sem("turned"), r.sem("xT_ready")
        multiplied, biased = r.sem("multiplied"), r.sem("biased")
        stored = [r.sem(f"stored{i}") for i in range(2)]
        with nc.Block() as block:
            @block.sync
            def _(s):
                for i, n in enumerate("qkv"):
                    s.dma_start(W[:, :, i * D:(i + 1) * D], w["W" + n].rearrange("(c p) n -> p c n", p=P)).then_inc(w_loaded, 16)
                    s.dma_start(brow[:, i * D:(i + 1) * D], w["b" + n].partition_broadcast(P)).then_inc(w_loaded, 16)
                with s.Fori(0, NB // U) as it:
                    for k in range(U):
                        n = it * U + k
                        s.wait_ge(biased, n + 1)
                        for i in range(2):
                            s.dma_start(kv[i][bass.ds(n * P, P), :], rows[:, k % 2, i * D:(i + 1) * D]).then_inc(stored[k % 2], 16)
                for i in range(2):
                    s.wait_ge(stored[i], 32 * (NB // 2))

            @block.scalar
            def _(a):
                with a.Fori(0, NB // U) as it:
                    for k in range(U):
                        n = it * U + k
                        a.wait_ge(turned, n + 1)
                        a.activation(stage[:, k % 2, :], xc[:, n, :], ACT.Copy, scale=rstd[:, bass.ds(n, 1)]).then_inc(staged, 1)
                        a.wait_ge(turned, n + 3)
                        a.wait_ge(multiplied, n + 1)
                        a.activation(xT[:, k % 2, :], psT[k % 2][:], ACT.Copy).then_inc(xT_ready, 1)

            @block.tensor
            def _(t):
                t.sem_inc(turned, 2)
                t.sem_inc(multiplied, 2)
                t.wait_ge(w_ready, 1)
                with t.Fori(0, NB // U) as it:
                    for k in range(U):
                        n = it * U + k
                        t.wait_ge(staged, n + 1)
                        t.transpose(psT[k % 2][:, 0:P], stage[:, k % 2, 0:P], c["ident"][:])
                        t.transpose(psT[k % 2][:, P:D], stage[:, k % 2, P:D], c["ident"][:]).then_inc(turned, 1)
                        t.wait_ge(xT_ready, n + 1)
                        t.wait_ge(biased, n)
                        for h in range(2):
                            t.matmul(psqk[k % 2][:], xT[:, k % 2, h * P:(h + 1) * P], W[:, h, 0:2 * D], start=h == 0, stop=h == 1)
                        for h in range(2):
                            m = t.matmul(psv[k % 2][:], xT[:, k % 2, h * P:(h + 1) * P], W[:, h, 2 * D:3 * D], start=h == 0, stop=h == 1)
                        m.then_inc(multiplied, 1)

            @block.vector
            def _(v):
                v.wait_ge(w_loaded, 96)
                v.tensor_scalar(W[:, :, 0:D], W[:, :, 0:D], HD ** -0.5, None, ALU.mult)
                v.tensor_scalar(brow[:, 0:D], brow[:, 0:D], HD ** -0.5, None, ALU.mult).then_inc(w_ready, 1)
                v.wait_ge(w_ready, 1)
                with v.Fori(0, NB // U) as it:
                    for k in range(U):
                        n = it * U + k
                        v.wait_ge(multiplied, n + 3)
                        v.wait_ge(stored[k % 2], it * (16 * U) + 32 * (k // 2))
                        v.tensor_tensor(q_sb[:, n, :], psqk[k % 2][:, 0:D], brow[:, 0:D], ALU.add)
                        v.tensor_tensor(rows[:, k % 2, 0:D], psqk[k % 2][:, D:2 * D], brow[:, D:2 * D], ALU.add)
                        v.tensor_tensor(rows[:, k % 2, D:2 * D], psv[k % 2][:], brow[:, 2 * D:3 * D], ALU.add).then_inc(biased, 1)


def sort_edges(nc, c, g, key_tile, idx_tile, key_flat, sorted_rows, first):
    with Region(nc, g.name + "_sort") as r:
        key_i = r.sb("key_i", [P, g.tiles], I32)
        idx_i = r.sb("idx_i", [P, g.tiles], I32)
        key = r.sb("key_f", [P, g.tiles])
        lo_i = r.sb("lo_i", [P, g.tiles], I32)
        lo = r.sb("lo", [P, g.tiles])
        hi = r.sb("hi", [P, g.tiles])
        blank = r.sb("blank", [P, g.slots])
        zero = r.sb("zero", [P, KEYS_HI])
        iota = r.sb("iota_b", [P, P], BF16)
        tri = r.sb("tri", [P, P])
        triT = r.sb("triT", [P, P])
        identb = r.sb("identb", [P, P], BF16)
        hi_one = [r.sb(f"hi_one{i}", [P, HALF, KEYS_HI], BF16) for i in range(2)]
        lo_one = [r.sb(f"lo_one{i}", [P, HALF, P], BF16) for i in range(2)]
        prefix = r.sb("prefix", [KEYS_HI, P])
        start = r.sb("start", [KEYS_HI, P])
        total = r.sb("total", [KEYS_HI, 4])
        whole = r.sb("whole", [KEYS_HI, 1], I32)
        row_key = [r.sb(f"row_key{i}", [P, HALF * P], I32) for i in range(2)]
        hiT = [r.sb(f"hiT{i}", [KEYS_HI, P]) for i in range(2)]
        count = [r.sb(f"count{i}", [KEYS_HI, P]) for i in range(2)]
        rank = [r.sb(f"rank{i}", [P, HALF]) for i in range(2)]
        before = [r.sb(f"before{i}", [P, HALF]) for i in range(2)]
        place = [r.sb(f"place{i}", [P, HALF], I32) for i in range(2)]
        pay = [r.sb(f"pay{i}", [P, HALF, 4]) for i in range(2)]
        junk = r.sb("junk", [P, 2, HALF, P])
        ps_count = r.ps("ps_count", [KEYS_HI, P])
        ps_base = r.ps("ps_base", [KEYS_HI, 1])
        ps_hiT = [r.ps(f"ps_hiT{i}", [KEYS_HI, P]) for i in range(2)]
        ps_at = [r.ps(f"ps_at{i}", [P, P]) for i in range(2)]
        loaded, filled, split, made = r.sem("loaded"), r.sem("filled"), r.sem("split"), r.sem("made")
        one_hot, counted = r.sem("one_hot"), r.sem("counted")
        with nc.Block() as block:
            @block.sync
            def _(s):
                s.dma_start(key_i[:], key_tile).then_inc(loaded, 16)
                s.dma_start(idx_i[:], idx_tile).then_inc(loaded, 16)
                s.wait_ge(filled, 3)
                flat = sorted_rows.rearrange("(q p j) f -> q p (j f)", q=4, p=P)
                for q in range(4):
                    s.dma_start(flat[q], blank[:]).then_inc(loaded, 16)
                s.wait_ge(loaded, 6 * 16)

            @block.gpsimd
            def _(e):
                e.memset(blank[:], 0.0).then_inc(filled, 1)
                e.wait_ge(filled, 1)
                e.memset(blank[:].rearrange("p (j f) -> p j f", f=4)[:, :, 1:2], -1.0).then_inc(filled, 1)
                e.memset(blank[:].rearrange("p (j f) -> p j f", f=4)[:, :, 2:3], -1.0).then_inc(filled, 1)
                e.memset(tri[:], 1.0).then_inc(made, 1)
                e.memset(triT[:], 1.0).then_inc(made, 1)
                e.memset(pay[0][:], 0.0).then_inc(made, 1)
                e.memset(pay[1][:], 0.0).then_inc(made, 1)
                e.memset(zero[:], 0.0).then_inc(made, 1)
                e.wait_ge(made, 5)
                e.affine_select(out=tri[:], in_=tri[:], compare_op=ALU.is_gt, fill=0.0, base=0,
                                pattern=[[-1, P]], channel_multiplier=1).then_inc(made, 1)
                e.affine_select(out=triT[:], in_=triT[:], compare_op=ALU.is_gt, fill=0.0, base=0,
                                pattern=[[1, P]], channel_multiplier=-1).then_inc(made, 1)
                e.wait_ge(made, 7)

            @block.vector
            def _(v):
                v.wait_ge(loaded, 96)
                v.tensor_copy(key[:], key_i[:])
                v.tensor_single_scalar(lo_i[:], key_i[:], P - 1, ALU.bitwise_and).then_inc(split, 1)
                v.tensor_copy(iota[:], c["iota"][:])
                v.tensor_copy(identb[:], c["ident"][:])
                v.wait_ge(split, 1)
                v.tensor_copy(lo[:], lo_i[:]).then_inc(split, 1)
                v.wait_ge(split, 2)
                v.tensor_tensor(hi[:], key[:], lo[:], ALU.subtract).then_inc(split, 1)
                v.wait_ge(split, 3)
                v.tensor_scalar(hi[:], hi[:], 1.0 / P, None, ALU.mult).then_inc(split, 1)
                v.wait_ge(split, 4)
                with v.Fori(0, g.tiles // (2 * HALF)) as it:
                    for h in range(2):
                        m = it * 2 + h
                        v.wait_ge(counted, m + 1)
                        v.tensor_tensor(hi_one[h][:], iota[:, 0:KEYS_HI].unsqueeze(1).to_broadcast([P, HALF, KEYS_HI]),
                                        hi[:, bass.ds(m * HALF, HALF)].unsqueeze(2).to_broadcast([P, HALF, KEYS_HI]), ALU.is_equal)
                        v.tensor_tensor(lo_one[h][:], iota[:].unsqueeze(1).to_broadcast([P, HALF, P]),
                                        lo[:, bass.ds(m * HALF, HALF)].unsqueeze(2).to_broadcast([P, HALF, P]), ALU.is_equal).then_inc(one_hot, 1)

            @block.tensor
            def _(t):
                t.sem_inc(counted, 2)
                t.wait_ge(made, 7)
                t.matmul(ps_count[:], zero[:], tri[:], start=True, stop=True, skip_group_check=True)
                with t.Fori(0, g.tiles // (2 * HALF)) as it:
                    for h in range(2):
                        m = it * 2 + h
                        t.wait_ge(one_hot, m + 1)
                        for j in range(HALF):
                            i = t.matmul(ps_count[:], hi_one[h][:, j, :], lo_one[h][:, j, :], start=False, stop=True, skip_group_check=True)
                        i.then_inc(counted, 1)
        with Region(nc, g.name + "_sort") as r2, nc.Block() as block:
            done, based = r2.sem("start_done"), r2.sem("based")

            @block.vector
            def _(v):
                ch = Chain(v, done)
                ch.inc(v.tensor_copy(prefix[:], ps_count[:]))
                ch.wait()
                ch.inc(v.memset(start[:], 0.0))
                ch.wait()
                ch.inc(v.tensor_tensor_scan(prefix[:], prefix[:], start[:], 0.0, ALU.add, ALU.add))
                ch.wait()
                ch.inc(v.tensor_scalar(total[:, 0:1], prefix[:, P - 1:P], float(STEP * P - 1), None, ALU.add))
                ch.wait()
                ch.inc(v.tensor_copy(whole[:], total[:, 0:1]))
                ch.wait()
                ch.inc(v.tensor_scalar(whole[:], whole[:], SHIFT, SHIFT, ALU.logical_shift_right, ALU.logical_shift_left))
                ch.wait()
                ch.inc(v.tensor_copy(total[:, 2:3], whole[:]))
                ch.inc(v.tensor_scalar(total[:, 3:4], c["col"][0:KEYS_HI, :], float(BLOCKS), FAR, ALU.is_ge, ALU.mult))
                ch.wait()
                v.wait_ge(based, 1)
                ch.inc(v.tensor_tensor(total[:, 0:1], ps_base[:], total[:, 3:4], ALU.add))
                ch.inc(v.tensor_copy(start[:, 1:P], prefix[:, 0:P - 1]))
                ch.wait()
                ch.inc(v.tensor_scalar(start[:], start[:], total[:, 0:1], None, ALU.add))
                ch.inc(v.tensor_copy(first[:], total[:, 0:1]))
                ch.wait()

            @block.tensor
            def _(t):
                t.wait_ge(done, 8)
                t.matmul(ps_base[:], triT[0:KEYS_HI, 0:KEYS_HI], total[:, 2:3], start=True, stop=True).then_inc(based, 1)

        with Region(nc, g.name + "_sort") as r3, nc.Block() as block:
            row_loaded = [r3.sem(f"row_loaded{i}") for i in range(2)]
            ranked, hots = r3.sem("ranked"), r3.sem("hots")
            flipped, hiT_ready = r3.sem("flipped"), r3.sem("hiT_ready")
            updated, count_ready, found, selected = r3.sem("updated"), r3.sem("count_ready"), r3.sem("found"), r3.sem("selected")
            placed, paid, issued = r3.sem("placed"), r3.sem("paid"), r3.sem("issued")
            scattered = [r3.sem(f"scattered{i}") for i in range(2)]
            LOOPS = g.tiles // (2 * HALF)

            @block.sync
            def _(s):
                with s.Fori(0, LOOPS) as it:
                    for h in range(2):
                        m = it * 2 + h
                        s.wait_ge(ranked, m + 1)
                        s.dma_start(row_key[h][:], key_flat[bass.ds(m * HALF * P, HALF * P)].partition_broadcast(P)).then_inc(row_loaded[h], 16)

            @block.vector
            def _(v):
                v.sem_inc(ranked, 2)
                v.sem_inc(selected, 2)
                with v.Fori(0, LOOPS) as it:
                    for h in range(2):
                        m = it * 2 + h
                        v.wait_ge(updated, m * HALF + 1)
                        v.tensor_tensor(hi_one[h][:], iota[:, 0:KEYS_HI].unsqueeze(1).to_broadcast([P, HALF, KEYS_HI]),
                                        hi[:, bass.ds(m * HALF, HALF)].unsqueeze(2).to_broadcast([P, HALF, KEYS_HI]), ALU.is_equal)
                        v.tensor_tensor(lo_one[h][:], iota[:].unsqueeze(1).to_broadcast([P, HALF, P]),
                                        lo[:, bass.ds(m * HALF, HALF)].unsqueeze(2).to_broadcast([P, HALF, P]), ALU.is_equal).then_inc(hots, 1)
                        v.wait_ge(row_loaded[h], it * 16 + 16)
                        v.wait_ge(placed, m + 1)
                        for j in range(HALF):
                            i = v.scalar_tensor_tensor(out=junk[:, 0, j, :], in0=row_key[h][:, j * P:(j + 1) * P], scalar=key[:, bass.ds(m * HALF + j, 1)],
                                                       in1=tri[:], op0=ALU.is_equal, op1=ALU.mult, accum_out=rank[h][:, j:j + 1])
                        i.then_inc(ranked, 1)
                        for j in range(HALF):
                            n = m * HALF + j
                            v.wait_ge(found, n + 1)
                            v.scalar_tensor_tensor(out=junk[:, 1, j, :], in0=ps_at[j % 2][:], scalar=0.0, in1=lo_one[h][:, j, :],
                                                   op0=ALU.add, op1=ALU.mult, accum_out=before[h][:, j:j + 1]).then_inc(selected, 1)
                        v.wait_ge(selected, m * HALF + HALF + 2)
                        v.wait_ge(ranked, m + 3)
                        v.wait_ge(scattered[h], it * 16 * HALF)
                        v.tensor_tensor(place[h][:], before[h][:], rank[h][:], ALU.add).then_inc(placed, 1)

            @block.scalar
            def _(a):
                a.sem_inc(hiT_ready, 2)
                with a.Fori(0, LOOPS) as it:
                    for h in range(2):
                        m = it * 2 + h
                        a.wait_ge(scattered[h], it * 16 * HALF)
                        a.activation(pay[h][:, :, 0], idx_i[:, bass.ds(m * HALF, HALF)], ACT.Copy)
                        a.activation(pay[h][:, :, 1], key[:, bass.ds(m * HALF, HALF)], ACT.Copy)
                        a.activation(pay[h][:, :, 2], lo[:, bass.ds(m * HALF, HALF)], ACT.Copy).then_inc(paid, 1)
                        for j in range(HALF):
                            n = m * HALF + j
                            a.wait_ge(flipped, n + 1)
                            a.wait_ge(found, n)
                            a.activation(hiT[j % 2][:], ps_hiT[j % 2][:], ACT.Copy).then_inc(hiT_ready, 1)
                            a.wait_ge(updated, n + 1 + HALF)
                            a.activation(count[j % 2][:], ps_count[:], ACT.Copy).then_inc(count_ready, 1)

            @block.tensor
            def _(t):
                t.matmul(ps_count[:], c["ident"][0:KEYS_HI, 0:KEYS_HI], start[:], start=True, stop=True, skip_group_check=True).then_inc(updated, HALF + 1)
                with t.Fori(0, LOOPS) as it:
                    for h in range(2):
                        m = it * 2 + h
                        t.wait_ge(hots, m + 1)
                        for j in range(HALF):
                            n = m * HALF + j
                            t.wait_ge(hiT_ready, n + 1)
                            t.matmul(ps_hiT[j % 2][:], hi_one[h][:, j, :], identb[:], start=True, stop=True).then_inc(flipped, 1)
                            t.wait_ge(hiT_ready, n + 3)
                            t.wait_ge(count_ready, n + 1)
                            t.wait_ge(selected, n + 1)
                            t.matmul(ps_at[j % 2][:], hiT[j % 2][:], count[j % 2][:], start=True, stop=True).then_inc(found, 1)
                            t.matmul(ps_count[:], hi_one[h][:, j, :], lo_one[h][:, j, :], start=False, stop=True, skip_group_check=True).then_inc(updated, 1)

            @block.gpsimd
            def _(e):
                e.sem_inc(placed, 2)
                last = e.to_reg(g.pos - 1)
                with e.Fori(0, LOOPS) as it:
                    for h in range(2):
                        m = it * 2 + h
                        e.wait_ge(placed, m + 3)
                        e.wait_ge(paid, m + 1)
                        e.sem_inc(issued, 1)
                        for j in range(HALF):
                            e.indirect_dma_start(out=sorted_rows, out_offset=bass.IndirectOffsetOnAxis(ap=place[h][:, j:j + 1], axis=0),
                                                 in_=pay[h][:, j, :], in_offset=None, bounds_check=last, oob_is_err=False).then_inc(scattered[h], 16)
                for h in range(2):
                    e.wait_ge(scattered[h], 16 * HALF * LOOPS)


def unpack(nc, c, g, sorted_rows, first, key_line, lo_line, idx, lo, item_block):
    C, T = g.chunks, g.chunk
    with Region(nc, g.name + "_unpack") as r:
        rows = [r.sb(f"rows{i}", [T, P, 4]) for i in range(2)]
        part = [r.sb(f"part{i}", [T, 3, P]) for i in range(2)]
        at = r.sb("at", [KEYS_HI, g.items])
        at_i = r.sb("at_i", [KEYS_HI, g.items], I32)
        counted = r.sb("counted_b", [KEYS_HI, P])
        ps = [r.ps(f"ps_part{i}", [P, 2, T]) for i in range(2)]
        ps_item = r.ps("ps_item", [P, 2, 512])
        loaded = [r.sem(f"rows_loaded{i}") for i in range(2)]
        lined = [r.sem(f"lined{i}") for i in range(2)]
        apart, turned, copied = r.sem("apart"), r.sem("parts_turned"), r.sem("copied")
        item, item_made, item_sum = r.sem("item"), r.sem("item_made"), r.sem("item_sum")
        half = g.items // 2
        with nc.Block() as block:
            @block.sync
            def _(s):
                for k in range(C):
                    if k >= 2:
                        s.wait_ge(apart, k - 1)
                    s.dma_start(rows[k % 2][:], sorted_rows[k * T * P:(k + 1) * T * P, :].rearrange("(t p) f -> t p f", p=P)).then_inc(loaded[k % 2], 16)
                    if k >= 1:
                        s.wait_ge(apart, k)
                        for i, line in enumerate((key_line, lo_line)):
                            s.dma_start(line[(k - 1) * T * P:k * T * P].rearrange("(t p) -> t p", p=P), part[(k - 1) % 2][:, i + 1, :]).then_inc(lined[(k - 1) % 2], 16)
                s.wait_ge(apart, C)
                for i, line in enumerate((key_line, lo_line)):
                    s.dma_start(line[(C - 1) * T * P:C * T * P].rearrange("(t p) -> t p", p=P), part[(C - 1) % 2][:, i + 1, :]).then_inc(lined[(C - 1) % 2], 16)
                s.wait_ge(lined[0], 32 * ((C + 1) // 2))
                s.wait_ge(lined[1], 32 * (C // 2))

            @block.vector
            def _(v):
                for k in range(C):
                    v.wait_ge(loaded[k % 2], 16 * (k // 2 + 1))
                    if k >= 2:
                        v.wait_ge(lined[k % 2], 32 * (k // 2))
                        v.wait_ge(turned, k - 1)
                    v.tensor_copy(part[k % 2][:], rows[k % 2][:, :, 0:3].rearrange("t p f -> t f p")).then_inc(apart, 1)
                v.wait_ge(item, 3)
                v.tensor_copy(at[:], at_i[:]).then_inc(item_made, 1)
                v.wait_ge(item_made, 1)
                v.tensor_scalar(at[:], at[:], first[:, 0:1], None, ALU.is_ge).then_inc(item_made, 1)
                v.wait_ge(item_sum, 1)
                v.tensor_copy(item_block[:].rearrange("p (a b) -> p a b", a=2), ps_item[0:1, :, 0:half]).then_inc(item_made, 1)
                v.wait_ge(item_made, 3)

            @block.gpsimd
            def _(e):
                e.iota(at_i[:], pattern=[[STEP * P, g.items]], base=0, channel_multiplier=0).then_inc(item, 1)
                e.memset(counted[:], 1.0).then_inc(item, 1)
                e.wait_ge(item, 2)
                e.affine_select(out=counted[:], in_=counted[:], compare_op=ALU.is_gt, fill=0.0, base=0,
                                pattern=[[0, P]], channel_multiplier=1).then_inc(item, 1)

            @block.tensor
            def _(t):
                for k in range(C):
                    t.wait_ge(apart, k + 1)
                    if k >= 2:
                        t.wait_ge(copied, 2 * (k - 1))
                    t.transpose(ps[k % 2][:, 0, :], part[k % 2][:, 0, :], c["ident"][0:T, 0:T])
                    t.transpose(ps[k % 2][:, 1, :], part[k % 2][:, 2, :], c["ident"][0:T, 0:T]).then_inc(turned, 1)
                t.wait_ge(item_made, 2)
                for a in range(2):
                    i = t.matmul(ps_item[:, a, 0:half], counted[:], at[:, a * half:(a + 1) * half], start=True, stop=True)
                i.then_inc(item_sum, 1)

            @block.scalar
            def _(a):
                for k in range(C):
                    a.wait_ge(turned, k + 1)
                    a.activation(idx[:, k * T:(k + 1) * T], ps[k % 2][:, 0, :], ACT.Copy).then_inc(copied, 1)
                    a.activation(lo[:, k * T:(k + 1) * T], ps[k % 2][:, 1, :], ACT.Copy).then_inc(copied, 1)
                a.wait_ge(copied, 2 * C)


def attention_scores(nc, c, g, idx, lo_line, item_block, q_sb, k_rows, scores):
    H = AI // 2
    TH = H * STEP
    LOOPS = g.items // AI
    with Region(nc, "score") as r:
        slot = [r.sb(f"slot{i}", [P, TH], I32) for i in range(2)]
        k_got = [r.sb(f"k_got{i}", [P, STEP * D]) for i in range(AI)]
        row_lo = [r.sb(f"row_lo{i}", [P, TH * P]) for i in range(2)]
        hot = [r.sb(f"hot{i}", [P, TH * P]) for i in range(2)]
        prod = [r.sb(f"prod{i}", [P, STEP * D]) for i in range(2)]
        s_tile = r.sb("s_tile", [P, 2 * TH, HEADS])
        s_line = r.sb("s_line", [P, P])
        ps_q = [r.ps(f"ps_q{i}", [P, STEP * D]) for i in range(2)]
        ps_s = r.ps("ps_s", [P, P])
        slotted, hot_ready, expanded = r.sem("slotted"), r.sem("hot_ready"), r.sem("expanded")
        got = [r.sem(f"got{i}") for i in range(AI)]
        row_loaded = [r.sem(f"row_loaded{i}") for i in range(2)]
        multiplied, reduced, turned, lined, stored = r.sem("multiplied"), r.sem("reduced"), r.sem("turned"), r.sem("lined"), r.sem("stored")
        issued = r.sem("issued")
        out = scores.rearrange("t h p -> (t h) p")
        with nc.Block() as block:
            @block.sync
            def _(s):
                with s.Fori(0, LOOPS) as it:
                    for h in range(2):
                        m = it * 2 + h
                        s.wait_ge(hot_ready, m + 1)
                        s.dma_start(row_lo[h][:], lo_line[bass.ds(m * TH * P, TH * P)].partition_broadcast(P)).then_inc(row_loaded[h], 16)
                    s.wait_ge(lined, it + 1)
                    s.dma_start(out[bass.ts(it, P), :], s_line[:]).then_inc(stored, 16)
                s.wait_ge(stored, 16 * LOOPS)

            @block.scalar
            def _(a):
                with a.Fori(0, LOOPS) as it:
                    a.wait_ge(turned, it + 1)
                    a.wait_ge(stored, it * 16)
                    a.activation(s_line[:], ps_s[:], ACT.Copy).then_inc(lined, 1)

            @block.gpsimd
            def _(e):
                with e.Fori(0, LOOPS) as it:
                    for k in range(AI):
                        n = it * AI + k
                        if k % H == 0:
                            h = k // H
                            for i in range(H):
                                e.wait_ge(got[h * H + i], it * 16 * STEP)
                            e.tensor_copy(slot[h][:], idx[:, bass.ds((it * 2 + h) * TH, TH)]).then_inc(slotted, 1)
                            e.wait_ge(slotted, it * 2 + h + 1)
                        e.wait_ge(multiplied, n + 1)
                        e.sem_inc(issued, 1)
                        for j in range(STEP):
                            e.indirect_dma_start(out=k_got[k][:, j * D:(j + 1) * D], out_offset=None, in_=k_rows,
                                                 in_offset=bass.IndirectOffsetOnAxis(ap=slot[k // H][:, k % H * STEP + j:k % H * STEP + j + 1], axis=0)).then_inc(got[k], 16)

            @block.tensor
            def _(t):
                with t.Fori(0, LOOPS) as it:
                    for k in range(AI):
                        n = it * AI + k
                        b = t.value_load(item_block[:, bass.ds(n, 1)], min_val=0, max_val=BLOCKS - 1)
                        t.wait_ge(hot_ready, it * 2 + k // H + 3)
                        t.wait_ge(multiplied, n - 2 + 1 + AI)
                        for j in range(STEP):
                            e = (k % H * STEP + j) * P
                            i = t.matmul(ps_q[k % 2][:, j * D:(j + 1) * D], hot[k // H][:, e:e + P], q_sb[:, b, :], start=True, stop=True)
                        i.then_inc(expanded, 1)
                    t.wait_ge(reduced, (it + 1) * AI)
                    t.wait_ge(lined, it)
                    t.transpose(ps_s[:], s_tile[:].rearrange("p t h -> p (t h)"), c["ident"][:]).then_inc(turned, 1)

            @block.vector
            def _(v):
                v.sem_inc(hot_ready, 2)
                v.sem_inc(multiplied, AI)
                with v.Fori(0, LOOPS) as it:
                    for k in range(AI):
                        n = it * AI + k
                        if k % H == 0:
                            h = k // H
                            v.wait_ge(row_loaded[h], it * 16 + 16)
                            v.wait_ge(expanded, n)
                            v.tensor_scalar(hot[h][:], row_lo[h][:], c["col"][:, 0:1], None, ALU.is_equal).then_inc(hot_ready, 1)
                        v.wait_ge(got[k], it * 16 * STEP + 16 * STEP)
                        v.wait_ge(expanded, n + 1)
                        v.wait_ge(reduced, n)
                        v.tensor_tensor(prod[k % 2][:], k_got[k][:], ps_q[k % 2][:], ALU.mult).then_inc(multiplied, 1)
                        if k == 0:
                            v.wait_ge(turned, it)
                        v.wait_ge(multiplied, n + 1 + AI)
                        v.tensor_reduce(s_tile[:, k * STEP:(k + 1) * STEP, :], prod[k % 2][:].rearrange("p (t d h) -> p t h d", t=STEP, h=HEADS),
                                        AX.X, ALU.add).then_inc(reduced, 1)


def segment_softmax(nc, c, g, heads, scores, key_line, probs):
    R, W = g.chunk, g.chunks * P
    with Region(nc, g.name + "_softmax") as r:
        key = r.sb("key", [R, W + 2])
        cut = r.sb("cut", [R, W + 1])
        s = r.sb("s", [R, heads, W])
        f = r.sb("f", [R, heads, W])
        back = r.sb("back", [R, W])
        ends = r.sb("ends", [P, 2, P])
        over = r.sb("over", [P, P + 1])
        carry = r.sb("carry", [R, heads])
        ps_ends = r.ps("ps_ends", [P, 2, P])
        ps_carry = r.ps("ps_carry", [P, P])
        loaded, bare, done, turned, sent, stored = r.sem("loaded"), r.sem("bare"), r.sem("done"), r.sem("turned"), r.sem("sent"), r.sem("stored")
        ready, raised = r.sem("ready"), r.sem("raised")
        with nc.Block() as block:
            @block.sync
            def _(q):
                q.wait_ge(bare, 2)
                line = key_line.rearrange("(p w) -> p w", w=W)
                q.dma_start(key[:, 1:W + 1], line).then_inc(loaded, 16)
                q.dma_start(key[1:R, 0:1], line[0:R - 1, W - 1:W], allow_slow_non_contiguous=True).then_inc(loaded, 16)
                q.dma_start(key[0:R - 1, W + 1:W + 2], line[1:R, 0:1], allow_slow_non_contiguous=True).then_inc(loaded, 16)
                for h in range(heads):
                    q.dma_start(s[:, h, :].rearrange("r (t p) -> r t p", p=P), scores.rearrange("(r t) h p -> h r t p", r=R)[h]).then_inc(loaded, 16)
                for h in range(heads):
                    q.wait_ge(raised, h + 1)
                    q.dma_start(probs.rearrange("(r t) h p -> h r t p", r=R)[h], f[:, h, :].rearrange("r (t p) -> r t p", p=P)).then_inc(stored, 16)
                q.wait_ge(stored, 16 * heads)

            @block.tensor
            def _(t):
                for i in range(2):
                    t.wait_ge(sent, 2 * i + 1)
                    t.transpose(ps_ends[:, 0, :], ends[:, 0, :], c["ident"][:])
                    t.transpose(ps_ends[:, 1, :], ends[:, 1, :], c["ident"][:]).then_inc(turned, 1)
                    t.wait_ge(sent, 2 * i + 2)
                    t.transpose(ps_carry[:], over[:, 0:P] if i == 0 else over[:, 1:P + 1], c["ident"][:]).then_inc(turned, 1)

            @block.scalar
            def _(a):
                for h in range(heads):
                    a.wait_ge(ready, h + 1)
                    a.activation(f[:, h, :], f[:, h, :], ACT.Exp).then_inc(raised, 1)

            @block.vector
            def _(v):
                v.memset(key[:, 0:1], -2.0).then_inc(bare, 1)
                v.memset(key[:, W + 1:W + 2], -2.0).then_inc(bare, 1)
                ch = Chain(v, done)
                ch.inc(v.memset(ends[:], 0.0))
                ch.inc(v.memset(over[:], LOWEST))
                v.wait_ge(loaded, 16 * (3 + heads))
                ch.inc(v.tensor_tensor(cut[:], key[:, 0:W + 1], key[:, 1:W + 2], ALU.is_equal))
                ch.wait()
                ch.inc(v.tensor_scalar(cut[:], cut[:], -1.0, -LOWEST, ALU.add, ALU.mult))
                ch.wait()
                for i in range(2):
                    fwd = i == 0
                    edge = cut[:, 0:W] if fwd else cut[:, 1:W + 1][:, ::-1]

                    def run(ap):
                        return ap if fwd else ap[:, ::-1]
                    for h in range(heads):
                        src = s[:, h, :] if fwd else f[:, h, :]
                        ch.inc(v.tensor_tensor_scan(run(back[:]), edge, run(src), LOWEST, ALU.add, ALU.max))
                        ch.wait()
                        ch.inc(v.tensor_copy(ends[0:R, 0, h:h + 1], back[:, W - 1:W] if fwd else back[:, 0:1]))
                        ch.wait()
                    ch.inc(v.tensor_reduce(carry[:, 0:1], edge, AX.X, ALU.min))
                    ch.wait()
                    v.tensor_copy(ends[0:R, 1, 0:heads], carry[:, 0:1].to_broadcast([R, heads])).then_inc(sent, 1)
                    v.wait_ge(turned, 2 * i + 1)
                    ch.inc(v.tensor_copy(back[0:heads, 0:R], ps_ends[0:heads, 1, 0:R]))
                    ch.inc(v.memset(over[:], LOWEST))
                    ch.wait()
                    to = over[0:heads, 1:R + 1] if fwd else over[0:heads, 0:R][:, ::-1]
                    v.tensor_tensor_scan(to, run(back[0:heads, 0:R]), run(ps_ends[0:heads, 0, 0:R]), LOWEST, ALU.add, ALU.max).then_inc(sent, 1)
                    v.wait_ge(turned, 2 * i + 2)
                    ch.inc(v.tensor_copy(carry[:], ps_carry[0:R, 0:heads]))
                    ch.wait()
                    for h in range(heads):
                        src = s[:, h, :] if fwd else f[:, h, :]
                        ch.inc(v.tensor_tensor_scan(run(f[:, h, :]), edge, run(src), carry[:, h:h + 1], ALU.add, ALU.max))
                    ch.wait()
                for h in range(heads):
                    v.tensor_tensor(f[:, h, :], s[:, h, :], f[:, h, :], ALU.subtract).then_inc(ready, 1)


def attention_sum(nc, c, g, idx, lo, item_block, v_rows, probs, acc):
    H = AI // 2
    TH = H * STEP
    LOOPS = g.items // AI
    A = D + HEADS
    with Region(nc, "sum") as r:
        slot = [r.sb(f"slot{i}", [P, TH], I32) for i in range(2)]
        v_got = [r.sb(f"v_got{i}", [P, STEP * D]) for i in range(AI)]
        p_line = r.sb("p_line", [P, P])
        p_tile = [r.sb(f"p_tile{i}", [P, TH, HEADS]) for i in range(2)]
        hot = [r.sb(f"hot{i}", [P, STEP, P]) for i in range(2)]
        w = [r.sb(f"w{i}", [P, STEP, A]) for i in range(2)]
        ps_p = r.ps("ps_p", [P, 2 * TH, HEADS])
        ps_a = [r.ps(f"ps_a{i}", [P, A]) for i in range(2)]
        slotted, p_loaded, turned, tiled = r.sem("slotted"), r.sem("p_loaded"), r.sem("turned"), r.sem("tiled")
        got = [r.sem(f"got{i}") for i in range(AI)]
        weighted, summed, added, issued, beside = r.sem("weighted"), r.sem("summed"), r.sem("added"), r.sem("issued"), r.sem("beside")
        src = probs.rearrange("t h p -> (t h) p")
        with nc.Block() as block:
            @block.sync
            def _(s):
                with s.Fori(0, LOOPS) as it:
                    s.wait_ge(turned, it)
                    s.dma_start(p_line[:], src[bass.ts(it, P), :]).then_inc(p_loaded, 16)

            @block.scalar
            def _(a):
                with a.Fori(0, LOOPS) as it:
                    a.wait_ge(turned, it + 1)
                    for h in range(2):
                        a.wait_ge(weighted, it * AI + (h + 1) * H)
                        a.activation(p_tile[h][:], ps_p[:, h * TH:(h + 1) * TH, :], ACT.Copy).then_inc(tiled, 1)
                    a.wait_ge(tiled, it * 2 + 2)
                    for k in range(AI):
                        n = it * AI + k
                        a.wait_ge(summed, n + 1)
                        a.activation(w[k % 2][:, :, D:A], p_tile[k // H][:, k % H * STEP:(k % H + 1) * STEP, :], ACT.Copy).then_inc(beside, 1)

            @block.gpsimd
            def _(e):
                with e.Fori(0, LOOPS) as it:
                    for k in range(AI):
                        n = it * AI + k
                        if k % H == 0:
                            h = k // H
                            for i in range(H):
                                e.wait_ge(got[h * H + i], it * 16 * STEP)
                            e.tensor_copy(slot[h][:], idx[:, bass.ds((it * 2 + h) * TH, TH)]).then_inc(slotted, 1)
                            e.wait_ge(slotted, it * 2 + h + 1)
                        e.wait_ge(weighted, n + 1)
                        e.sem_inc(issued, 1)
                        for j in range(STEP):
                            e.indirect_dma_start(out=v_got[k][:, j * D:(j + 1) * D], out_offset=None, in_=v_rows,
                                                 in_offset=bass.IndirectOffsetOnAxis(ap=slot[k // H][:, k % H * STEP + j:k % H * STEP + j + 1], axis=0)).then_inc(got[k], 16)

            @block.tensor
            def _(t):
                t.sem_inc(summed, 2)
                with t.Fori(0, LOOPS) as it:
                    t.wait_ge(p_loaded, it * 16 + 16)
                    t.wait_ge(tiled, it * 2)
                    t.transpose(ps_p[:].rearrange("p t h -> p (t h)"), p_line[:], c["ident"][:]).then_inc(turned, 1)
                    for k in range(AI):
                        n = it * AI + k
                        t.wait_ge(weighted, n + 1 + AI)
                        t.wait_ge(beside, n + 1)
                        t.wait_ge(added, n + 1)
                        for j in range(STEP):
                            i = t.matmul(ps_a[k % 2][:], hot[k % 2][:, j, :], w[k % 2][:, j, :], start=j == 0, stop=j == STEP - 1)
                        i.then_inc(summed, 1)

            @block.vector
            def _(v):
                v.memset(acc[:], 0.0).then_inc(added, 1)
                v.wait_ge(added, 1)
                v.sem_inc(added, 1)
                v.sem_inc(weighted, AI)
                with v.Fori(0, LOOPS) as it:
                    for k in range(AI):
                        n = it * AI + k
                        v.wait_ge(summed, n + 1)
                        v.tensor_tensor(hot[k % 2][:], c["iota"][:].unsqueeze(1).to_broadcast([P, STEP, P]),
                                        lo[:, bass.ds(n * STEP, STEP)].unsqueeze(2).to_broadcast([P, STEP, P]), ALU.is_equal)
                        v.wait_ge(got[k], it * 16 * STEP + 16 * STEP)
                        if k % H == 0:
                            v.wait_ge(tiled, it * 2 + k // H + 1)
                        v.tensor_tensor(w[k % 2][:, :, 0:D].rearrange("p t (d h) -> p t d h", h=HEADS), v_got[k][:].rearrange("p (t d h) -> p t d h", t=STEP, h=HEADS),
                                        p_tile[k // H][:, k % H * STEP:(k % H + 1) * STEP, :].unsqueeze(2).to_broadcast([P, STEP, HD, HEADS]), ALU.mult).then_inc(weighted, 1)
                        b = v.value_load(item_block[:, bass.ds(n, 1)], min_val=0, max_val=BLOCKS - 1)
                        v.wait_ge(summed, n + 3)
                        v.wait_ge(added, n + 2)
                        v.tensor_tensor(acc[:, b, :], acc[:, b, :], ps_a[k % 2][:], ALU.add).then_inc(added, 1)


def attention_out(nc, c, acc, w_out, b_out, x_sb):
    A = D + HEADS
    with Region(nc, "out") as r:
        W = r.sb("W", [P, 2, D])
        brow = r.sb("brow", [P, D])
        inv = r.sb("inv", [P, NB, HEADS])
        stage = r.sb("stage", [P, 2, D])
        yT = r.sb("yT", [P, 2, D])
        psT = [r.ps(f"psT{i}", [P, D]) for i in range(2)]
        ps_y = [r.ps(f"ps_y{i}", [P, D]) for i in range(2)]
        loaded, inverse, staged, turned = r.sem("loaded"), r.sem("inverse"), r.sem("staged"), r.sem("turned")
        yT_ready, multiplied, added = r.sem("yT_ready"), r.sem("multiplied"), r.sem("added")
        with nc.Block() as block:
            @block.sync
            def _(s):
                s.dma_start(W[:], w_out.rearrange("(c p) n -> p c n", p=P)).then_inc(loaded, 16)
                s.dma_start(brow[:], b_out.partition_broadcast(P)).then_inc(loaded, 16)
                s.wait_ge(loaded, 32)

            @block.vector
            def _(v):
                ch = Chain(v, inverse)
                ch.inc(v.tensor_scalar(inv[:], acc[:, :, D:A], 1e-30, None, ALU.max))
                ch.wait()
                ch.inc(v.reciprocal(inv[:], inv[:]))
                v.wait_ge(loaded, 32)
                ch.inc(v.tensor_tensor(x_sb[:], x_sb[:], brow[:].unsqueeze(1).to_broadcast([P, NB, D]), ALU.add))
                ch.wait()
                with v.Fori(0, NB // U) as it:
                    for k in range(U):
                        n = it * U + k
                        v.wait_ge(turned, n + 1)
                        v.tensor_tensor(stage[:, k % 2, :].rearrange("p (d h) -> p d h", h=HEADS), acc[:, n, 0:D].rearrange("p (d h) -> p d h", h=HEADS),
                                        inv[:, n, :].unsqueeze(1).to_broadcast([P, HD, HEADS]), ALU.mult).then_inc(staged, 1)
                        v.wait_ge(multiplied, n + 3)
                        v.tensor_tensor(x_sb[:, n, :], x_sb[:, n, :], ps_y[k % 2][:], ALU.add).then_inc(added, 1)

            @block.tensor
            def _(t):
                t.sem_inc(turned, 2)
                t.sem_inc(multiplied, 2)
                t.wait_ge(loaded, 32)
                with t.Fori(0, NB // U) as it:
                    for k in range(U):
                        n = it * U + k
                        t.wait_ge(staged, n + 1)
                        t.transpose(psT[k % 2][:, 0:P], stage[:, k % 2, 0:P], c["ident"][:])
                        t.transpose(psT[k % 2][:, P:D], stage[:, k % 2, P:D], c["ident"][:]).then_inc(turned, 1)
                        t.wait_ge(yT_ready, n + 1)
                        t.wait_ge(added, n)
                        for h in range(2):
                            m = t.matmul(ps_y[k % 2][:], yT[:, k % 2, h * P:(h + 1) * P], W[:, h, :], start=h == 0, stop=h == 1)
                        m.then_inc(multiplied, 1)

            @block.scalar
            def _(a):
                with a.Fori(0, NB // U) as it:
                    for k in range(U):
                        n = it * U + k
                        a.wait_ge(turned, n + 3)
                        a.wait_ge(multiplied, n + 1)
                        a.activation(yT[:, k % 2, :], psT[k % 2][:], ACT.Copy).then_inc(yT_ready, 1)


def gat_rows(nc, c, xc, rstd, w_gat, att_src, att_dst, xT_all, table, a_dst):
    F = GH * EX
    with Region(nc, "gat_rows") as r:
        W = r.sb("W", [P, 2, F])
        att = r.sb("att", [P, 2, F])
        rows = r.sb("rows", [P, NB, GROW])
        prod = r.sb("prod", [P, 2, NB, F])
        stage = r.sb("stage", [P, 2, D])
        xT = r.sb("xT", [P, 2, D])
        psT = [r.ps(f"psT{i}", [P, D]) for i in range(2)]
        ps_h = [r.ps(f"ps_h{i}", [P, F]) for i in range(2)]
        loaded, staged, turned, xT_ready = r.sem("loaded"), r.sem("staged"), r.sem("turned"), r.sem("xT_ready")
        kept, multiplied, taken, scored, stored = r.sem("kept"), r.sem("multiplied"), r.sem("taken"), r.sem("scored"), r.sem("stored")
        with nc.Block() as block:
            @block.sync
            def _(s):
                s.dma_start(W[:], w_gat.rearrange("(c p) n -> p c n", p=P)).then_inc(loaded, 16)
                s.dma_start(att[:, 0, :], att_src.rearrange("h e -> (h e)").partition_broadcast(P)).then_inc(loaded, 16)
                s.dma_start(att[:, 1, :], att_dst.rearrange("h e -> (h e)").partition_broadcast(P)).then_inc(loaded, 16)
                s.wait_ge(scored, 4)
                s.dma_start(table.rearrange("(b p) f -> p b f", p=P), rows[:]).then_inc(stored, 16)
                s.wait_ge(stored, 16)

            @block.scalar
            def _(a):
                with a.Fori(0, NB // U) as it:
                    for k in range(U):
                        n = it * U + k
                        a.wait_ge(turned, n + 1)
                        a.activation(stage[:, k % 2, :], xc[:, n, :], ACT.Copy, scale=rstd[:, bass.ds(n, 1)]).then_inc(staged, 1)
                        a.wait_ge(turned, n + 3)
                        a.wait_ge(multiplied, n + 1)
                        a.wait_ge(kept, n + 1)
                        a.activation(xT[:, k % 2, :], psT[k % 2][:], ACT.Copy).then_inc(xT_ready, 1)

            @block.tensor
            def _(t):
                t.sem_inc(turned, 2)
                t.sem_inc(multiplied, 2)
                t.wait_ge(loaded, 48)
                with t.Fori(0, NB // U) as it:
                    for k in range(U):
                        n = it * U + k
                        t.wait_ge(staged, n + 1)
                        t.transpose(psT[k % 2][:, 0:P], stage[:, k % 2, 0:P], c["ident"][:])
                        t.transpose(psT[k % 2][:, P:D], stage[:, k % 2, P:D], c["ident"][:]).then_inc(turned, 1)
                        t.wait_ge(xT_ready, n + 1)
                        t.wait_ge(taken, n + 1)
                        for h in range(2):
                            m = t.matmul(ps_h[k % 2][:], xT[:, k % 2, h * P:(h + 1) * P], W[:, h, :], start=h == 0, stop=h == 1)
                        m.then_inc(multiplied, 1)

            @block.vector
            def _(v):
                v.sem_inc(kept, 2)
                v.sem_inc(taken, 2)
                with v.Fori(0, NB // U) as it:
                    for k in range(U):
                        n = it * U + k
                        v.wait_ge(xT_ready, n + 1)
                        v.tensor_copy(xT_all[:, :, bass.ds(n * P, P)], xT[:, k % 2, :].rearrange("p (c n) -> p c n", c=2)).then_inc(kept, 1)
                        v.wait_ge(multiplied, n + 3)
                        v.tensor_copy(rows[:, n, 0:F], ps_h[k % 2][:]).then_inc(taken, 1)
                v.wait_ge(taken, NB + 2)
                for i in range(2):
                    v.tensor_tensor(prod[:, i], rows[:, :, 0:F], att[:, i, :].unsqueeze(1).to_broadcast([P, NB, F]), ALU.mult).then_inc(scored, 1)
                v.wait_ge(scored, 2)
                for i, to in enumerate((rows[:, :, F:GROW], a_dst[:])):
                    v.tensor_reduce(to, prod[:, i].rearrange("p b (h e) -> p b h e", e=EX), AX.X, ALU.add).then_inc(scored, 1)
                v.wait_ge(scored, 4)


def gat_scores(nc, c, g, idx, lo_line, item_block, table, a_dst, kept_rows, scores):
    F = GH * EX
    H = GI // 2
    TH = H * STEP
    LOOPS = g.items // GI
    R = 2 * TH * GH
    with Region(nc, "gat_score") as r:
        slot = [r.sb(f"slot{i}", [P, TH], I32) for i in range(2)]
        rows = [r.sb(f"rows{i}", [P, TH, GROW]) for i in range(2)]
        hot = [r.sb(f"hot{i}", [P, TH * P]) for i in range(2)]
        e_sum = r.sb("e_sum", [P, 2, TH, GH])
        s_tile = r.sb("s_tile", [P, 2 * TH, GH])
        s_line = r.sb("s_line", [R, P])
        ps_d = [r.ps(f"ps_d{i}", [P, TH, GH]) for i in range(2)]
        ps_s = r.ps("ps_s", [R, P])
        clamped, slotted, hot_ready, expanded = r.sem("clamped"), r.sem("slotted"), r.sem("hot_ready"), r.sem("expanded")
        got = [r.sem(f"got{i}") for i in range(2)]
        row_loaded = [r.sem(f"row_loaded{i}") for i in range(2)]
        summed, leaked, turned, lined, stored = r.sem("summed"), r.sem("leaked"), r.sem("turned"), r.sem("lined"), r.sem("stored")
        kept = [r.sem(f"kept{i}") for i in range(2)]
        issued = r.sem("issued")
        out = scores.rearrange("t h p -> (t h) p")
        with nc.Block() as block:
            @block.sync
            def _(s):
                with s.Fori(0, LOOPS) as it:
                    for h in range(2):
                        m = it * 2 + h
                        s.wait_ge(expanded, m + 1)
                        s.dma_start(hot[h][:], lo_line[bass.ds(m * TH * P, TH * P)].partition_broadcast(P)).then_inc(row_loaded[h], 16)
                    s.wait_ge(lined, it + 1)
                    s.dma_start(out[bass.ds(it * R, R), :], s_line[:]).then_inc(stored, 16)
                s.wait_ge(stored, 16 * LOOPS)

            @block.scalar
            def _(a):
                with a.Fori(0, LOOPS) as it:
                    for h in range(2):
                        m = it * 2 + h
                        a.wait_ge(got[h], it * 16 * TH + 16 * TH)
                        a.dma_start(kept_rows[bass.ds(m * P, P), :], rows[h][:].rearrange("p t f -> p (t f)")).then_inc(kept[h], 16)
                    a.wait_ge(turned, it + 1)
                    a.wait_ge(stored, it * 16)
                    a.activation(s_line[:], ps_s[:], ACT.Copy).then_inc(lined, 1)
                for h in range(2):
                    a.wait_ge(kept[h], 16 * LOOPS)

            @block.gpsimd
            def _(e):
                e.wait_ge(clamped, 1)
                with e.Fori(0, LOOPS) as it:
                    for h in range(2):
                        m = it * 2 + h
                        e.wait_ge(kept[h], it * 16)
                        e.wait_ge(summed, m + 1)
                        e.wait_ge(got[h], it * 16 * TH)
                        e.tensor_copy(slot[h][:], idx[:, bass.ds(m * TH, TH)]).then_inc(slotted, 1)
                        e.wait_ge(slotted, m + 1)
                        e.sem_inc(issued, 1)
                        for j in range(TH):
                            e.indirect_dma_start(out=rows[h][:, j, :], out_offset=None, in_=table,
                                                 in_offset=bass.IndirectOffsetOnAxis(ap=slot[h][:, j:j + 1], axis=0)).then_inc(got[h], 16)

            @block.tensor
            def _(t):
                t.sem_inc(expanded, 2)
                with t.Fori(0, LOOPS) as it:
                    for h in range(2):
                        m = it * 2 + h
                        t.wait_ge(hot_ready, m + 1)
                        t.wait_ge(summed, m + 1)
                        for k in range(H):
                            b = t.value_load(item_block[:, bass.ds(m * H + k, 1)], min_val=0, max_val=BLOCKS - 1)
                            for j in range(k * STEP, (k + 1) * STEP):
                                i = t.matmul(ps_d[h][:, j, :], hot[h][:, j * P:(j + 1) * P], a_dst[:, b, :], start=True, stop=True)
                        i.then_inc(expanded, 1)
                    t.wait_ge(leaked, it * 2 + 2)
                    t.wait_ge(lined, it)
                    t.transpose(ps_s[:], s_tile[:].rearrange("p t h -> p (t h)"), c["ident"][:]).then_inc(turned, 1)

            @block.vector
            def _(v):
                v.tensor_scalar(idx[:], idx[:], N - 1, None, ALU.min).then_inc(clamped, 1)
                v.sem_inc(summed, 2)
                with v.Fori(0, LOOPS) as it:
                    for h in range(2):
                        m = it * 2 + h
                        v.wait_ge(row_loaded[h], it * 16 + 16)
                        v.tensor_scalar(hot[h][:], hot[h][:], c["col"][:, 0:1], None, ALU.is_equal).then_inc(hot_ready, 1)
                        v.wait_ge(got[h], it * 16 * TH + 16 * TH)
                        v.wait_ge(expanded, m + 3)
                        v.tensor_tensor(e_sum[:, h], rows[h][:, :, F:GROW], ps_d[h][:], ALU.add).then_inc(summed, 1)
                        v.wait_ge(summed, m + 3)
                        if h == 0:
                            v.wait_ge(turned, it)
                        v.scalar_tensor_tensor(out=s_tile[:, h * TH:(h + 1) * TH, :], in0=e_sum[:, h], scalar=0.2, in1=e_sum[:, h],
                                               op0=ALU.mult, op1=ALU.max).then_inc(leaked, 1)


def gat_sum(nc, c, g, lo, item_block, kept_rows, probs, acc):
    F = GH * EX
    H = GI // 2
    TH = H * STEP
    LOOPS = g.items // GI
    R = 2 * TH * GH
    with Region(nc, "gat_sum") as r:
        p_line = r.sb("p_line", [R, P])
        hot = [r.sb(f"hot{i}", [P, TH, P]) for i in range(2)]
        rows = [r.sb(f"rows{i}", [P, TH, GROW]) for i in range(2)]
        w = [r.sb(f"w{i}", [P, TH, GROW]) for i in range(2)]
        ps_p = r.ps("ps_p", [P, 2 * TH, GH])
        ps_a = [r.ps(f"ps_a{i}", [P, H, GROW]) for i in range(2)]
        p_loaded, turned, weighted, summed, added = r.sem("p_loaded"), r.sem("turned"), r.sem("weighted"), r.sem("summed"), r.sem("added")
        row_loaded = [r.sem(f"row_loaded{i}") for i in range(2)]
        src = probs.rearrange("t h p -> (t h) p")
        with nc.Block() as block:
            @block.sync
            def _(s):
                with s.Fori(0, LOOPS) as it:
                    s.wait_ge(turned, it)
                    s.dma_start(p_line[:], src[bass.ds(it * R, R), :]).then_inc(p_loaded, 16)
                    for h in range(2):
                        m = it * 2 + h
                        s.wait_ge(weighted, m + 1)
                        s.dma_start(rows[h][:].rearrange("p t f -> p (t f)"), kept_rows[bass.ds(m * P, P), :]).then_inc(row_loaded[h], 16)
                s.wait_ge(p_loaded, 16 * LOOPS)

            @block.tensor
            def _(t):
                t.sem_inc(summed, 2)
                t.sem_inc(weighted, 2)
                with t.Fori(0, LOOPS) as it:
                    t.wait_ge(p_loaded, it * 16 + 16)
                    t.wait_ge(weighted, it * 2 + 2)
                    t.transpose(ps_p[:].rearrange("p t h -> p (t h)"), p_line[:], c["ident"][0:R, 0:R]).then_inc(turned, 1)
                    for h in range(2):
                        m = it * 2 + h
                        t.wait_ge(weighted, m + 3)
                        t.wait_ge(added, m * H + 1)
                        for k in range(H):
                            for j in range(STEP):
                                i = t.matmul(ps_a[h][:, k, :], hot[h][:, k * STEP + j, :], w[h][:, k * STEP + j, :], start=j == 0, stop=j == STEP - 1)
                        i.then_inc(summed, 1)

            @block.vector
            def _(v):
                v.memset(acc[:], 0.0).then_inc(added, 1)
                with v.Fori(0, LOOPS) as it:
                    for h in range(2):
                        m = it * 2 + h
                        v.wait_ge(summed, m + 1)
                        v.tensor_tensor(hot[h][:], c["iota"][:].unsqueeze(1).to_broadcast([P, TH, P]),
                                        lo[:, bass.ds(m * TH, TH)].unsqueeze(2).to_broadcast([P, TH, P]), ALU.is_equal)
                        v.wait_ge(turned, it + 1)
                        v.wait_ge(row_loaded[h], it * 16 + 16)
                        p = ps_p[:, h * TH:(h + 1) * TH, :]
                        v.tensor_tensor(w[h][:, :, 0:F].rearrange("p t (h e) -> p t h e", e=EX), rows[h][:, :, 0:F].rearrange("p t (h e) -> p t h e", e=EX),
                                        p.unsqueeze(3).to_broadcast([P, TH, GH, EX]), ALU.mult)
                        v.tensor_copy(w[h][:, :, F:GROW], p).then_inc(weighted, 1)
                        for k in range(H):
                            b = v.value_load(item_block[:, bass.ds(m * H + k, 1)], min_val=0, max_val=BLOCKS - 1)
                            if k == 0:
                                v.wait_ge(summed, m + 3)
                            v.wait_ge(added, m * H + k + 1)
                            v.tensor_tensor(acc[:, b, :], acc[:, b, :], ps_a[h][:, k, :], ALU.add).then_inc(added, 1)
                v.wait_ge(added, LOOPS * GI + 1)


def route(nc, c, acc, b_gat, gamma, beta, gate):
    F = GH * EX
    with Region(nc, "route") as r:
        par = r.sb("par", [P, 3, F])
        inv = r.sb("inv", [P, NB, GH])
        y = r.sb("y", [P, NB, F])
        y2 = r.sb("y2", [P, NB, F])
        mean = r.sb("mean", [P, NB])
        var = r.sb("var", [P, NB])
        sc = r.sb("sc", [P, NB, EX])
        less = r.sb("less", [P, NB, EX, EX])
        same = r.sb("same", [P, NB, EX, EX])
        lower = r.sb("lower", [P, EX, EX])
        top = r.sb("top", [P, NB])
        loaded, done, low, vary, root, shifted, raised = (r.sem(n) for n in ("loaded", "done", "low", "vary", "root", "shifted", "raised"))
        with nc.Block() as block:
            @block.sync
            def _(s):
                for i, a in enumerate((b_gat, gamma, beta)):
                    s.dma_start(par[:, i, :], a.partition_broadcast(P)).then_inc(loaded, 16)
                s.wait_ge(loaded, 48)

            @block.gpsimd
            def _(e):
                e.memset(lower[:], 1.0).then_inc(low, 1)
                e.wait_ge(low, 1)
                e.affine_select(out=lower[:], in_=lower[:], compare_op=ALU.is_gt, fill=0.0, base=0,
                                pattern=[[1, EX], [-1, EX]], channel_multiplier=0).then_inc(low, 1)

            @block.scalar
            def _(a):
                a.wait_ge(vary, 1)
                a.activation(var[:], var[:], ACT.Sqrt).then_inc(root, 1)
                a.wait_ge(shifted, 1)
                a.activation(gate[:], gate[:], ACT.Exp).then_inc(raised, 1)

            @block.vector
            def _(v):
                ch = Chain(v, done)

                def step(i):
                    ch.inc(i)
                    ch.wait()

                def rows(ap):
                    return ap.unsqueeze(1).to_broadcast([P, NB, F])

                def each(ap, n):
                    return ap.unsqueeze(2).to_broadcast([P, NB, n])
                step(v.tensor_scalar(inv[:], acc[:, :, F:GROW], 1e-16, None, ALU.add))
                step(v.reciprocal(inv[:], inv[:]))
                step(v.tensor_tensor(y[:].rearrange("p b (h e) -> p b h e", e=EX), acc[:, :, 0:F].rearrange("p b (h e) -> p b h e", e=EX),
                                     inv[:].unsqueeze(3).to_broadcast([P, NB, GH, EX]), ALU.mult))
                v.wait_ge(loaded, 48)
                step(v.tensor_tensor(y[:], y[:], rows(par[:, 0, :]), ALU.add))
                step(v.tensor_reduce(mean[:], y[:], AX.X, ALU.add))
                step(v.tensor_scalar(mean[:], mean[:], 1.0 / F, None, ALU.mult))
                step(v.tensor_tensor(y[:], y[:], each(mean[:], F), ALU.subtract))
                step(v.tensor_tensor(y2[:], y[:], y[:], ALU.mult))
                step(v.tensor_reduce(var[:], y2[:], AX.X, ALU.add))
                v.tensor_scalar(var[:], var[:], 1.0 / F, EPS, ALU.mult, ALU.add).then_inc(vary, 1)
                v.wait_ge(root, 1)
                step(v.reciprocal(var[:], var[:]))
                step(v.tensor_tensor(y[:], y[:], each(var[:], F), ALU.mult))
                step(v.tensor_tensor(y[:], y[:], rows(par[:, 1, :]), ALU.mult))
                step(v.tensor_tensor(y[:], y[:], rows(par[:, 2, :]), ALU.add))
                step(v.tensor_reduce(sc[:], y[:].rearrange("p b (h e) -> p b e h", e=EX), AX.X, ALU.add))
                step(v.tensor_scalar(sc[:], sc[:], 1.0 / GH, None, ALU.mult))
                step(v.tensor_reduce(top[:], sc[:], AX.X, ALU.max))
                v.tensor_tensor(gate[:], sc[:], each(top[:], EX), ALU.subtract).then_inc(shifted, 1)
                other = sc[:].unsqueeze(2).to_broadcast([P, NB, EX, EX])
                own = sc[:].unsqueeze(3).to_broadcast([P, NB, EX, EX])
                step(v.tensor_tensor(less[:], other, own, ALU.is_gt))
                step(v.tensor_tensor(same[:], other, own, ALU.is_equal))
                v.wait_ge(low, 2)
                step(v.tensor_tensor(same[:], same[:], lower[:].unsqueeze(1).to_broadcast([P, NB, EX, EX]), ALU.mult))
                step(v.tensor_tensor(less[:], less[:], same[:], ALU.add))
                step(v.tensor_reduce(sc[:], less[:], AX.X, ALU.add))
                step(v.tensor_scalar(sc[:], sc[:], 1.5, None, ALU.is_lt))
                v.wait_ge(raised, 1)
                step(v.tensor_tensor(gate[:], gate[:], sc[:], ALU.mult))
                step(v.tensor_reduce(top[:], gate[:], AX.X, ALU.add))
                step(v.reciprocal(top[:], top[:]))
                step(v.tensor_tensor(gate[:], gate[:], each(top[:], EX), ALU.mult))


FB = 5
FN = FB * P // 2


def experts(nc, c, xT_all, gate, w1, b1, w2, b2, x_sb, out):
    FC = FF // P
    with Region(nc, "ffn") as r:
        W1 = r.sb("W1", [P, EX, 2, FF])
        W2 = r.sb("W2", [P, EX, FC, D])
        B1 = r.sb("B1", [P, EX, FC])
        B2 = r.sb("B2", [1, EX, D])
        ones = r.sb("ones", [1, P])
        hid = [r.sb(f"hid{i}", [P, FC, FB * P]) for i in range(2)]
        ps1 = [r.ps(f"ps1_{i}", [P, FN]) for i in range(4)]
        ps2 = [r.ps(f"ps2_{i}", [P, D]) for i in range(4)]
        loaded, one, first, active, second, added, stored = (r.sem(n) for n in ("loaded", "one", "first", "active", "second", "added", "stored"))
        G = NB // FB
        M1, M2 = EX * FC * 2, EX * FB
        with nc.Block() as block:
            @block.sync
            def _(s):
                for e in range(EX):
                    s.dma_start(W1[:, e], w1[e].rearrange("(c p) f -> p c f", p=P)).then_inc(loaded, 16)
                    s.dma_start(W2[:, e], w2[e].rearrange("(c p) f -> p c f", p=P)).then_inc(loaded, 16)
                    s.dma_start(B1[:, e, :], b1[e].rearrange("(c p) -> p c", p=P), allow_slow_non_contiguous=True).then_inc(loaded, 16)
                s.dma_start(B2[:], b2.rearrange("e d -> (e d)").rearrange("(o f) -> o f", o=1).rearrange("o (e d) -> o e d", e=EX)).then_inc(loaded, 16)
                s.wait_ge(added, NB * EX + 4)
                s.dma_start(out[0:FULL * P, :].rearrange("(b p) d -> p b d", p=P), x_sb[:, 0:FULL, :]).then_inc(stored, 16)
                s.dma_start(out[FULL * P:N, :], x_sb[0:REST, FULL, :]).then_inc(stored, 16)
                s.wait_ge(stored, 32)

            @block.gpsimd
            def _(e):
                e.memset(ones[:], 1.0).then_inc(one, 1)

            @block.tensor
            def _(t):
                t.wait_ge(loaded, 16 * (3 * EX + 1))
                t.wait_ge(one, 1)
                with t.Fori(0, G) as it:
                    def up(e):
                        for q in range(FC * 2):
                            n = it * M1 + e * FC * 2 + q
                            f, s = divmod(q, 2)
                            t.wait_ge(active, n + 1)
                            for h in range(2):
                                i = t.matmul(ps1[q % 4][:], W1[:, e, h, f * P:(f + 1) * P], xT_all[:, h, bass.ds(it * FB * P + s * FN, FN)],
                                             start=h == 0, stop=h == 1)
                            i.then_inc(first, 1)

                    def down(e):
                        t.wait_ge(active, it * M1 + (e + 1) * FC * 2 + 4)
                        for b in range(FB):
                            n = it * M2 + e * FB + b
                            q = (e * FB + b) % 4
                            t.wait_ge(added, n + 1)
                            t.matmul(ps2[q][:], ones[:], B2[:, e, :], start=True, stop=False)
                            for f in range(FC):
                                i = t.matmul(ps2[q][:], hid[e % 2][:, f, b * P:(b + 1) * P], W2[:, e, f, :], start=False, stop=f == FC - 1)
                            i.then_inc(second, 1)
                    up(0)
                    for e in range(EX):
                        if e + 1 < EX:
                            up(e + 1)
                        down(e)

            @block.scalar
            def _(a):
                a.sem_inc(active, 4)
                a.wait_ge(loaded, 16 * (3 * EX + 1))
                with a.Fori(0, G) as it:
                    for e in range(EX):
                        a.wait_ge(second, it * M2 + (e + 1) * FB)
                        for q in range(FC * 2):
                            f, s = divmod(q, 2)
                            a.wait_ge(first, it * M1 + e * FC * 2 + q + 1)
                            a.activation(hid[e % 2][:, f, s * FN:(s + 1) * FN], ps1[q % 4][:], ACT.Gelu, bias=B1[:, e, f:f + 1]).then_inc(active, 1)

            @block.vector
            def _(v):
                v.sem_inc(second, 2 * FB)
                v.sem_inc(added, 4)
                with v.Fori(0, G) as it:
                    for e in range(EX):
                        for b in range(FB):
                            n = it * M2 + e * FB + b
                            q = (e * FB + b) % 4
                            v.wait_ge(second, n + 1 + 2 * FB)
                            if e:
                                v.wait_ge(added, n - FB + 1 + 4)
                            v.scalar_tensor_tensor(out=x_sb[:, it * FB + b, :], in0=ps2[q][:], scalar=gate[:, it * FB + b, e:e + 1],
                                                   in1=x_sb[:, it * FB + b, :], op0=ALU.mult, op1=ALU.add).then_inc(added, 1)


def program(nc, x, att_key_tile, att_idx_tile, att_key_flat, Wq, bq, Wk, bk, Wv, bv, Wo, bo,
            gat_key_tile, gat_idx_tile, gat_key_flat, W_gat, att_src, att_dst, b_gat, ln_gamma, ln_beta, W1, b1, W2, b2, out):
    def dram(name, shape, dt=F32):
        return nc.dram_tensor(name, shape, dt).ap()

    def ordered(r, g, key_tile, idx_tile, key_flat):
        n = g.name
        idx, lo = r.sb(n + "_idx", [P, g.slots], I32), r.sb(n + "_lo", [P, g.slots])
        block, first = r.sb(n + "_block", [1, g.items], I32), r.sb(n + "_first", [KEYS_HI, 1])
        rows, key_line, lo_line = dram(n + "_rows", (g.pos, 4)), dram(n + "_key_line", (g.pos,)), dram(n + "_lo_line", (g.pos,))
        sort_edges(nc, c, g, key_tile, idx_tile, key_flat, rows, first)
        unpack(nc, c, g, rows, first, key_line, lo_line, idx, lo, block)
        return idx, lo, block, key_line, lo_line

    with Region(nc, "top") as top:
        c = {"ident": top.sb("ident", [P, P]), "iota": top.sb("iota", [P, P]), "col": top.sb("col", [P, 1])}
        constants(nc, c)
        x_sb = top.sb("x_sb", [P, NB, D])
        with Region(nc, "att") as r0:
            idx, lo, block, key_line, lo_line = ordered(r0, ATT, att_key_tile, att_idx_tile, att_key_flat)
            scores, probs = dram("att_scores", (ATT.slots, HEADS, P)), dram("att_probs", (ATT.slots, HEADS, P))
            k_rows, v_rows = dram("k_rows", (NPAD, D)), dram("v_rows", (NPAD, D))
            with Region(nc, "q") as r:
                q_sb = r.sb("q_sb", [P, NB, D])
                with Region(nc, "centred") as r2:
                    xc, rstd = r2.sb("xc", [P, NB, D]), r2.sb("rstd", [P, NB])
                    normalise(nc, "norm0", x_sb, xc, rstd, x)
                    project(nc, c, xc, rstd, {"Wq": Wq, "bq": bq, "Wk": Wk, "bk": bk, "Wv": Wv, "bv": bv}, q_sb, (k_rows, v_rows))
                attention_scores(nc, c, ATT, idx, lo_line, block, q_sb, k_rows, scores)
            segment_softmax(nc, c, ATT, HEADS, scores, key_line, probs)
            with Region(nc, "sums") as r:
                acc = r.sb("acc", [P, NB, D + HEADS])
                attention_sum(nc, c, ATT, idx, lo, block, v_rows, probs, acc)
                attention_out(nc, c, acc, Wo, bo, x_sb)
        with Region(nc, "gat") as r:
            idx, lo, block, key_line, lo_line = ordered(r, GAT, gat_key_tile, gat_idx_tile, gat_key_flat)
            scores, probs = dram("gat_scores", (GAT.slots, GH, P)), dram("gat_probs", (GAT.slots, GH, P))
            table, kept_rows = dram("gat_table", (NPAD, GROW)), dram("gat_kept", (GAT.items // GI * 2 * P, GI // 2 * STEP * GROW))
            xT_all = r.sb("xT_all", [P, 2, NPAD])
            a_dst, gate = r.sb("a_dst", [P, NB, GH]), r.sb("gate", [P, NB, EX])
            acc = r.sb("acc", [P, NB, GROW])
            with Region(nc, "centred2") as r2:
                xc, rstd = r2.sb("xc", [P, NB, D]), r2.sb("rstd", [P, NB])
                normalise(nc, "norm1", x_sb, xc, rstd)
                gat_rows(nc, c, xc, rstd, W_gat, att_src, att_dst, xT_all, table, a_dst)
            gat_scores(nc, c, GAT, idx, lo_line, block, table, a_dst, kept_rows, scores)
            segment_softmax(nc, c, GAT, GH, scores, key_line, probs)
            gat_sum(nc, c, GAT, lo, block, kept_rows, probs, acc)
            route(nc, c, acc, b_gat, ln_gamma, ln_beta, gate)
            experts(nc, c, xT_all, gate, W1, b1, W2, b2, x_sb, out)


def kernel(x, src, dst, L0_gnn_Wq, L0_gnn_bq, L0_gnn_Wk, L0_gnn_bk, L0_gnn_Wv, L0_gnn_bv, L0_gnn_Wo, L0_gnn_bo,
           L0_ffn_W_gat, L0_ffn_att_src, L0_ffn_att_dst, L0_ffn_b_gat, L0_ffn_ln_gamma, L0_ffn_ln_beta,
           L0_ffn_W1, L0_ffn_b1, L0_ffn_W2, L0_ffn_b2, L0_ffn_edge_index):
    import numpy as np
    import concourse.bacc as bacc
    from concourse.bass_utils import run_bass_kernel_spmd

    def lists(g, key, idx):
        flat = np.full((2, g.tiles * P), 0, np.int32)
        flat[0, :] = PAD_KEY
        flat[0, 0:key.size] = key
        flat[1, 0:idx.size] = idx
        by_tile = [np.ascontiguousarray(a.reshape(g.tiles, P).T) for a in flat]
        return by_tile[0], by_tile[1], np.ascontiguousarray(flat[0])

    loops = np.arange(BLOCKS * P, dtype=np.int32)
    edge = np.asarray(L0_ffn_edge_index)
    att = lists(ATT, np.asarray(src), np.asarray(dst))
    gat = lists(GAT, np.concatenate([edge[1], loops]), np.concatenate([edge[0], loops]))
    given = [x, *att, L0_gnn_Wq, L0_gnn_bq, L0_gnn_Wk, L0_gnn_bk, L0_gnn_Wv, L0_gnn_bv, L0_gnn_Wo, L0_gnn_bo, *gat,
             L0_ffn_W_gat, L0_ffn_att_src, L0_ffn_att_dst, L0_ffn_b_gat, L0_ffn_ln_gamma, L0_ffn_ln_beta,
             L0_ffn_W1, L0_ffn_b1, L0_ffn_W2, L0_ffn_b2]
    nc = bacc.Bacc("TRN2", target_bir_lowering=False, num_devices=1)
    arrays, args = {}, []
    for i, a in enumerate(given):
        a = np.ascontiguousarray(a)
        arrays[f"in_{i}"] = a
        args.append(nc.dram_tensor(f"in_{i}", a.shape, mybir.dt.from_np(a.dtype), kind="ExternalInput").ap())
    out = nc.dram_tensor("out", (N, D), F32, kind="ExternalOutput").ap()
    program(nc, *args, out)
    got = run_bass_kernel_spmd(nc, [arrays], core_ids=[0])
    return got.results[0]["out"]
```

```python
from contextlib import ExitStack

import concourse.bass as bass
from concourse import mybir

F32 = mybir.dt.float32
BF16 = mybir.dt.bfloat16
I32 = mybir.dt.int32
ALU = mybir.AluOpType
ACT = mybir.ActivationFunctionType
AX = mybir.AxisListType
PE = mybir.EngineType.PE

P = 128
N = 6250
D = 256
NB = 50
NPAD = NB * P
FULL = N // P
REST = N - FULL * P
EPS = 1e-5
LOWEST = -1.0e38

HEADS = 8
HD = D // HEADS
GH = 4
EX = 4
GROW = GH * EX + GH
FF = 512
U = 10

BLOCKS = 49
KEYS_HI = 64
FAR = float(1 << 20)
PAD_KEY = KEYS_HI * P - 1
SHIFT = 8
STEP = (1 << SHIFT) // P
HALF = 8


class Edges:

    def __init__(self, name, edges, tiles, chunks, chunk):
        self.name, self.tiles, self.chunks, self.chunk = name, tiles, chunks, chunk
        self.slots = chunks * chunk
        self.items = self.slots // STEP
        self.pos = self.slots * P
        assert tiles * P >= edges and tiles % (2 * HALF) == 0 and self.slots % STEP == 0
        assert (edges + BLOCKS * (STEP * P - 1)) // (STEP * P) <= self.items


ATT = Edges("att", 200000, 1568, 13, 128)
GAT = Edges("gat", 131072 + BLOCKS * P, 1088, 12, 100)


H = 8
TH = H * STEP
assert TH * HEADS == P and ATT.items % (2 * H) == 0
GI = 12
GT = GI * STEP
assert GAT.items == 2 * GI * (NB // 2)


class Region:

    def __init__(self, nc, tag):
        self.nc, self.tag, self.ctx, self.sems = nc, tag, ExitStack(), []

    def __enter__(self):
        return self

    def __exit__(self, *e):
        if self.sems and e[0] is None:
            self.nc.clear_and_free_semaphores(self.sems)
            self.nc.all_engine_barrier()
        return self.ctx.__exit__(*e)

    def sb(self, name, shape, dt=F32):
        return self.ctx.enter_context(self.nc.sbuf_tensor(f"{self.tag}_{name}", shape, dt))

    def ps(self, name, shape, dt=F32):
        return self.ctx.enter_context(self.nc.psum_tensor(f"{self.tag}_{name}", shape, dt))

    def sem(self, name):
        self.sems.append(self.nc.alloc_semaphore(f"{self.tag}_{name}"))
        return self.sems[-1]


class Chain:

    def __init__(self, eng, sem, n=0):
        self.eng, self.sem, self.n = eng, sem, n

    def inc(self, instruction):
        instruction.then_inc(self.sem, 1)
        self.n += 1

    def wait(self):
        self.eng.wait_ge(self.sem, self.n)


def item_blocks(nc, engine, item_block, n, count):
    return nc.values_load_multi_w_load_instructions(item_block[:, bass.ds(n, count)], engines=(engine,), min_val=0, max_val=BLOCKS - 1)[1]


def quad_one_hots(v, hot, iota4, keys, tiles):
    shape = [P, tiles // 4, iota4.shape[1], 4]
    return v.tensor_tensor(hot, iota4.unsqueeze(1).to_broadcast(shape), keys.rearrange("p (q j) -> p q j", j=4).unsqueeze(2).to_broadcast(shape), ALU.is_equal)


def bc(ap, shape):
    return ap.to_broadcast(shape)


def constants(nc, c, x, x_sb, x_loaded):
    with Region(nc, "const") as r:
        made, padded = r.sem("const_made"), r.sem("padded")
        iota_i = r.sb("iota_i", [P, P], I32)
        col_i = r.sb("col_i", [P, 1], I32)
        with nc.Block() as block:
            @block.sync
            def _(s):
                s.wait_ge(padded, 1)
                s.dma_start(x_sb[:, 0:FULL, :], x[0:FULL * P, :].rearrange("(b p) d -> p b d", p=P)).then_inc(x_loaded, 16)
                s.dma_start(x_sb[0:REST, FULL, :], x[FULL * P:N, :]).then_inc(x_loaded, 16)

            @block.gpsimd
            def _(e):
                e.memset(x_sb[:, FULL:NB, :], 0.0).then_inc(padded, 1)
                e.memset(c["ident"][:], 0.0).then_inc(made, 1)
                e.iota(iota_i[:], pattern=[[1, P]], base=0, channel_multiplier=0).then_inc(made, 1)
                e.iota(col_i[:], pattern=[[1, 1]], base=0, channel_multiplier=1).then_inc(made, 1)
                e.wait_ge(made, 3)
                e.affine_select(out=c["ident"][:], in_=c["ident"][:], compare_op=ALU.not_equal, fill=1.0,
                                base=0, pattern=[[-1, P]], channel_multiplier=1).then_inc(made, 1)
                e.tensor_copy(c["iota"][:], iota_i[:]).then_inc(made, 1)
                e.tensor_copy(c["col"][:], col_i[:]).then_inc(made, 1)
                e.wait_ge(made, 6)


def normalise(nc, tag, x_sb, xc, rstd, x_loaded=None):
    SLAB = NB // 5
    with Region(nc, tag) as r:
        mean = r.sb("mean", [P, NB])
        sq = r.sb("sq", [P, 2, D])
        stat, centred, squared, spread, root = (r.sem(n) for n in ("stat", "centred", "squared", "spread", "root"))
        with nc.Block() as block:
            @block.vector
            def _(v):
                ch = Chain(v, stat)
                if x_loaded is not None:
                    v.wait_ge(x_loaded, 32)
                for b in range(0, NB, SLAB):
                    slab = slice(b, b + SLAB)
                    ch.inc(v.tensor_reduce(mean[:, slab], x_sb[:, slab, :], AX.X, ALU.add))
                    ch.wait()
                    ch.inc(v.tensor_scalar(mean[:, slab], mean[:, slab], 1.0 / D, None, ALU.mult))
                    ch.wait()
                    v.tensor_tensor(xc[:, slab, :], x_sb[:, slab, :], bc(mean[:, slab].unsqueeze(2), [P, SLAB, D]), ALU.subtract).then_inc(centred, 1)
                v.wait_ge(squared, NB)
                v.tensor_scalar(rstd[:], rstd[:], 1.0 / D, EPS, ALU.mult, ALU.add).then_inc(spread, 1)
                v.wait_ge(root, 1)
                ch.inc(v.reciprocal(rstd[:], rstd[:]))
                ch.wait()

            @block.scalar
            def _(a):
                for b in range(NB):
                    if b % SLAB == 0:
                        a.wait_ge(centred, b // SLAB + 1)
                    if b >= 2:
                        a.wait_ge(squared, b - 1)
                    a.activation(sq[:, b % 2, :], xc[:, b, :], ACT.Square, accum_out=rstd[:, b:b + 1]).then_inc(squared, 1)
                a.wait_ge(spread, 1)
                a.activation(rstd[:], rstd[:], ACT.Sqrt).then_inc(root, 1)


def project(nc, c, xc, rstd, w, q_sb, kv):
    with Region(nc, "proj") as r:
        W = r.sb("W", [P, 2, 3 * D])
        brow = r.sb("brow", [P, 3 * D])
        stage = r.sb("stage", [P, 2, D])
        xT = r.sb("xT", [P, 2, D])
        rows = r.sb("rows", [P, 2, 2 * D])
        psT = [r.ps(f"psT{i}", [P, D]) for i in range(2)]
        psqk = [r.ps(f"psqk{i}", [P, 2 * D]) for i in range(2)]
        psv = [r.ps(f"psv{i}", [P, D]) for i in range(2)]
        w_loaded, w_ready = r.sem("w_loaded"), r.sem("w_ready")
        staged, turned, xT_ready = r.sem("staged"), r.sem("turned"), r.sem("xT_ready")
        multiplied, biased = r.sem("multiplied"), r.sem("biased")
        stored, rows_free = r.sem("stored"), r.sem("rows_free")
        with nc.Block() as block:
            @block.sync
            def _(s):
                for i, n in enumerate("qkv"):
                    s.dma_start(W[:, :, i * D:(i + 1) * D], w["W" + n].rearrange("(c p) n -> p c n", p=P)).then_inc(w_loaded, 16)
                    s.dma_start(brow[:, i * D:(i + 1) * D], w["b" + n].partition_broadcast(P)).then_inc(w_loaded, 16)
                s.sem_inc(rows_free, 2)
                with s.Fori(0, NB // U) as it:
                    for k in range(U):
                        n = it * U + k
                        s.wait_ge(biased, n + 3)
                        for i in range(2):
                            s.dma_start(kv[i][bass.ds(n * P, P), :], rows[:, k % 2, i * D:(i + 1) * D]).then_inc(stored, 16)
                        s.wait_ge(stored, n * 32 + 32)
                        s.sem_inc(rows_free, 1)

            @block.scalar
            def _(a):
                def put_stage(n, k):
                    a.wait_ge(turned, n + 1)
                    a.activation(stage[:, k % 2, :], xc[:, n, :], ACT.Copy, scale=rstd[:, bass.ds(n, 1)]).then_inc(staged, 1)
                a.sem_inc(xT_ready, 2)
                with a.Fori(0, NB // U) as it:
                    put_stage(it * U, 0)
                    for k in range(U):
                        n = it * U + k
                        if k + 1 < U:
                            put_stage(n + 1, k + 1)
                        a.wait_ge(turned, n + 3)
                        a.wait_ge(multiplied, n + 1)
                        a.activation(xT[:, k % 2, :], psT[k % 2][:], ACT.Copy).then_inc(xT_ready, 1)

            @block.tensor
            def _(t):
                t.sem_inc(turned, 2)
                t.sem_inc(multiplied, 2)
                t.wait_ge(w_ready, 1)
                with t.Fori(0, NB // U) as it:
                    def turn(n, k):
                        t.wait_ge(staged, n + 1)
                        t.wait_ge(xT_ready, n + 1)
                        t.transpose(psT[k % 2][:, 0:P], stage[:, k % 2, 0:P], c["ident"][:])
                        t.transpose(psT[k % 2][:, P:D], stage[:, k % 2, P:D], c["ident"][:]).then_inc(turned, 1)
                    turn(it * U, 0)
                    for k in range(U):
                        n = it * U + k
                        if k + 1 < U:
                            turn(n + 1, k + 1)
                        t.wait_ge(xT_ready, n + 3)
                        t.wait_ge(biased, n + 1)
                        for h in range(2):
                            t.matmul(psqk[k % 2][:], xT[:, k % 2, h * P:(h + 1) * P], W[:, h, 0:2 * D], start=h == 0, stop=h == 1)
                        for h in range(2):
                            m = t.matmul(psv[k % 2][:], xT[:, k % 2, h * P:(h + 1) * P], W[:, h, 2 * D:3 * D], start=h == 0, stop=h == 1)
                        m.then_inc(multiplied, 1)

            @block.vector
            def _(v):
                v.wait_ge(w_loaded, 96)
                v.tensor_scalar(W[:, :, 0:D], W[:, :, 0:D], HD ** -0.5, None, ALU.mult)
                v.tensor_scalar(brow[:, 0:D], brow[:, 0:D], HD ** -0.5, None, ALU.mult).then_inc(w_ready, 1)
                v.wait_ge(w_ready, 1)
                v.sem_inc(biased, 2)
                with v.Fori(0, NB // U) as it:
                    for k in range(U):
                        n = it * U + k
                        v.wait_ge(multiplied, n + 3)
                        v.wait_ge(rows_free, n + 1)
                        v.tensor_tensor(q_sb[:, n, :], psqk[k % 2][:, 0:D], brow[:, 0:D], ALU.add)
                        v.tensor_tensor(rows[:, k % 2, 0:D], psqk[k % 2][:, D:2 * D], brow[:, D:2 * D], ALU.add)
                        v.tensor_tensor(rows[:, k % 2, D:2 * D], psv[k % 2][:], brow[:, 2 * D:3 * D], ALU.add).then_inc(biased, 1)


def sort_edges(nc, c, g, key_tile, idx_tile, key_flat, sorted_rows, first):
    with Region(nc, g.name + "_sort") as r:
        key_i = r.sb("key_i", [P, g.tiles], I32)
        idx_i = r.sb("idx_i", [P, g.tiles], I32)
        key = r.sb("key_f", [P, g.tiles])
        lo_i = r.sb("lo_i", [P, g.tiles], I32)
        hi_f = r.sb("hi_f", [P, g.tiles])
        lo = r.sb("lo", [P, g.tiles + HALF], BF16)
        hi = r.sb("hi", [P, g.tiles + HALF], BF16)
        blank = r.sb("blank", [P, g.slots])
        zero = r.sb("zero", [P, KEYS_HI])
        iota = r.sb("iota_b", [P, P], BF16)
        iota4 = r.sb("iota4", [P, P, 4], BF16)
        tri = r.sb("tri", [P, P])
        triT = r.sb("triT", [P, P])
        identb = r.sb("identb", [P, P], BF16)
        hi_one = [r.sb(f"hi_one{i}", [P, HALF, KEYS_HI], BF16) for i in range(2)]
        lo_one = [r.sb(f"lo_one{i}", [P, HALF, P], BF16) for i in range(2)]
        prefix = r.sb("prefix", [KEYS_HI, P])
        start = r.sb("start", [KEYS_HI, P])
        total = r.sb("total", [KEYS_HI, 4])
        whole = r.sb("whole", [KEYS_HI, 1], I32)
        row_key = [r.sb(f"row_key{i}", [P, HALF * P], I32) for i in range(2)]
        hiT = [r.sb(f"hiT{i}", [KEYS_HI, HALF * P]) for i in range(2)]
        count = [r.sb(f"count{i}", [KEYS_HI, P]) for i in range(4)]
        rank = [r.sb(f"rank{i}", [P, HALF]) for i in range(2)]
        before = [r.sb(f"before{i}", [P, HALF]) for i in range(2)]
        place = [r.sb(f"place{i}", [P, HALF], I32) for i in range(2)]
        pay = [r.sb(f"pay{i}", [P, HALF, 4]) for i in range(2)]
        junk = r.sb("junk", [P, 2, HALF, P])
        ps_count = r.ps("ps_count", [KEYS_HI, P])
        ps_base = r.ps("ps_base", [KEYS_HI, 1])
        ps_hiT = [r.ps(f"ps_hiT{i}", [KEYS_HI, 2 * P]) for i in range(2)]
        ps_at = [r.ps(f"ps_at{i}", [P, P]) for i in range(2)]
        loaded, filled, split, made = r.sem("loaded"), r.sem("filled"), r.sem("split"), r.sem("made")
        one_hot, counted = r.sem("one_hot"), r.sem("counted")

        def quads(one, keys):
            return one[:].rearrange("p t k -> p (t k)").rearrange("p (q k j) -> p q k j", k=keys, j=4)
        with nc.Block() as block:
            @block.sync
            def _(s):
                s.dma_start(key_i[:], key_tile).then_inc(loaded, 16)
                s.dma_start(idx_i[:], idx_tile).then_inc(loaded, 16)
                s.wait_ge(filled, 3)
                flat = sorted_rows.rearrange("(q p j) f -> q p (j f)", q=4, p=P)
                for q in range(4):
                    s.dma_start(flat[q], blank[:]).then_inc(loaded, 16)
                s.wait_ge(loaded, 6 * 16)

            @block.gpsimd
            def _(e):
                e.memset(blank[:], 0.0).then_inc(filled, 1)
                e.wait_ge(filled, 1)
                e.memset(blank[:].rearrange("p (j f) -> p j f", f=4)[:, :, 1:2], -1.0).then_inc(filled, 1)
                e.memset(blank[:].rearrange("p (j f) -> p j f", f=4)[:, :, 2:3], -1.0).then_inc(filled, 1)
                e.memset(tri[:], 1.0).then_inc(made, 1)
                e.memset(triT[:], 1.0).then_inc(made, 1)
                e.memset(pay[0][:], 0.0).then_inc(made, 1)
                e.memset(pay[1][:], 0.0).then_inc(made, 1)
                e.memset(zero[:], 0.0).then_inc(made, 1)
                e.wait_ge(made, 5)
                e.affine_select(out=tri[:], in_=tri[:], compare_op=ALU.is_gt, fill=0.0, base=0,
                                pattern=[[-1, P]], channel_multiplier=1).then_inc(made, 1)
                e.affine_select(out=triT[:], in_=triT[:], compare_op=ALU.is_gt, fill=0.0, base=0,
                                pattern=[[1, P]], channel_multiplier=-1).then_inc(made, 1)
                e.wait_ge(made, 7)

            @block.vector
            def _(v):
                v.wait_ge(loaded, 96)
                v.tensor_copy(key[:], key_i[:])
                v.tensor_single_scalar(lo_i[:], key_i[:], P - 1, ALU.bitwise_and).then_inc(split, 1)
                v.tensor_copy(iota[:], c["iota"][:])
                v.tensor_copy(iota4[:], c["iota"][:].unsqueeze(2).to_broadcast([P, P, 4]))
                v.tensor_copy(identb[:], c["ident"][:])
                v.memset(lo[:, g.tiles:g.tiles + HALF], 0.0)
                v.memset(hi[:, g.tiles:g.tiles + HALF], 0.0)
                v.wait_ge(split, 1)
                v.tensor_copy(lo[:, 0:g.tiles], lo_i[:]).then_inc(split, 1)
                v.wait_ge(split, 2)
                v.tensor_tensor(hi_f[:], key[:], lo[:, 0:g.tiles], ALU.subtract).then_inc(split, 1)
                v.wait_ge(split, 3)
                v.tensor_scalar(hi[:, 0:g.tiles], hi_f[:], 1.0 / P, None, ALU.mult).then_inc(split, 1)
                v.wait_ge(split, 4)
                with v.Fori(0, g.tiles // (2 * HALF)) as it:
                    for h in range(2):
                        m = it * 2 + h
                        v.wait_ge(counted, m + 1)
                        quad_one_hots(v, quads(hi_one[h], KEYS_HI), iota4[:, 0:KEYS_HI, :], hi[:, bass.ds(m * HALF, HALF)], HALF)
                        quad_one_hots(v, quads(lo_one[h], P), iota4[:], lo[:, bass.ds(m * HALF, HALF)], HALF).then_inc(one_hot, 1)

            @block.tensor
            def _(t):
                t.sem_inc(counted, 2)
                t.wait_ge(made, 7)
                t.matmul(ps_count[:], zero[:], tri[:], start=True, stop=True, skip_group_check=True)
                with t.Fori(0, g.tiles // (2 * HALF)) as it:
                    for h in range(2):
                        m = it * 2 + h
                        t.wait_ge(one_hot, m + 1)
                        for j in range(HALF):
                            i = t.matmul(ps_count[:], quads(hi_one[h], KEYS_HI)[:, j // 4, :, j % 4], quads(lo_one[h], P)[:, j // 4, :, j % 4],
                                         start=False, stop=True, skip_group_check=True)
                        i.then_inc(counted, 1)
        with Region(nc, g.name + "_sort") as r2, nc.Block() as block:
            done, based = r2.sem("start_done"), r2.sem("based")

            @block.vector
            def _(v):
                ch = Chain(v, done)
                ch.inc(v.tensor_copy(prefix[:], ps_count[:]))
                ch.wait()
                ch.inc(v.memset(start[:], 0.0))
                ch.wait()
                ch.inc(v.tensor_tensor_scan(prefix[:], prefix[:], start[:], 0.0, ALU.add, ALU.add))
                ch.wait()
                ch.inc(v.tensor_scalar(total[:, 0:1], prefix[:, P - 1:P], float(STEP * P - 1), None, ALU.add))
                ch.wait()
                ch.inc(v.tensor_copy(whole[:], total[:, 0:1]))
                ch.wait()
                ch.inc(v.tensor_scalar(whole[:], whole[:], SHIFT, SHIFT, ALU.logical_shift_right, ALU.logical_shift_left))
                ch.wait()
                ch.inc(v.tensor_copy(total[:, 2:3], whole[:]))
                ch.inc(v.tensor_scalar(total[:, 3:4], c["col"][0:KEYS_HI, :], float(BLOCKS), FAR, ALU.is_ge, ALU.mult))
                ch.wait()
                v.wait_ge(based, 1)
                ch.inc(v.tensor_tensor(total[:, 0:1], ps_base[:], total[:, 3:4], ALU.add))
                ch.inc(v.tensor_copy(start[:, 1:P], prefix[:, 0:P - 1]))
                ch.wait()
                ch.inc(v.tensor_scalar(start[:], start[:], total[:, 0:1], None, ALU.add))
                ch.inc(v.tensor_copy(first[:], total[:, 0:1]))
                ch.wait()

            @block.tensor
            def _(t):
                t.wait_ge(done, 8)
                t.matmul(ps_base[:], triT[0:KEYS_HI, 0:KEYS_HI], total[:, 2:3], start=True, stop=True).then_inc(based, 1)

        with Region(nc, g.name + "_rank") as r3, nc.Block() as block:
            row_loaded = [r3.sem(f"row_loaded{i}") for i in range(2)]
            ranked, hots = r3.sem("ranked"), r3.sem("hots")
            flipped, hiT_ready = r3.sem("flipped"), r3.sem("hiT_ready")
            updated, count_ready, found, selected = r3.sem("updated"), r3.sem("count_ready"), r3.sem("found"), r3.sem("selected")
            placed, paid, issued, sent = r3.sem("placed"), r3.sem("paid"), r3.sem("issued"), r3.sem("sent")
            scattered = [r3.sem(f"scattered{i}") for i in range(2)]
            LOOPS = g.tiles // (2 * HALF)

            @block.sync
            def _(s):
                s.sem_inc(sent, 2)
                with s.Fori(0, LOOPS) as it:
                    for h in range(2):
                        s.wait_ge(scattered[h], it * (16 * HALF) + 16 * HALF)
                        s.sem_inc(sent, 1)

            @block.vector
            def _(v):
                v.sem_inc(ranked, 2)
                v.sem_inc(selected, 2)
                v.sem_inc(placed, 2)

                def one_hots(to, m, q):
                    pair, at = slice(2 * q, 2 * q + 2), bass.ds(m * HALF + 2 * q, 2)
                    v.tensor_tensor(hi_one[to][:, pair, :], iota[:, 0:KEYS_HI].unsqueeze(1).to_broadcast([P, 2, KEYS_HI]),
                                    hi[:, at].unsqueeze(2).to_broadcast([P, 2, KEYS_HI]), ALU.is_equal)
                    v.tensor_tensor(lo_one[to][:, pair, :], iota[:].unsqueeze(1).to_broadcast([P, 2, P]),
                                    lo[:, at].unsqueeze(2).to_broadcast([P, 2, P]), ALU.is_equal).then_inc(hots, 1)
                for q in range(4):
                    one_hots(0, 0, q)
                with v.Fori(0, LOOPS) as it:
                    for h in range(2):
                        m = it * 2 + h
                        for j in range(HALF):
                            n = m * HALF + j
                            v.wait_ge(found, n + 1)
                            v.scalar_tensor_tensor(out=junk[:, 1, j, :], in0=ps_at[j % 2][:], scalar=0.0, in1=lo_one[h][:, j, :],
                                                   op0=ALU.add, op1=ALU.mult, accum_out=before[h][:, j:j + 1]).then_inc(selected, 1)
                            if j == 0:
                                v.wait_ge(updated, m * HALF + 1 + HALF)
                            if j < 4:
                                one_hots(1 - h, m + 1, j)
                            if j == 0:
                                v.wait_ge(row_loaded[h], it * 16 + 16)
                            i = v.scalar_tensor_tensor(out=junk[:, 0, j, :], in0=row_key[h][:, j * P:(j + 1) * P], scalar=key[:, bass.ds(m * HALF + j, 1)],
                                                       in1=tri[:], op0=ALU.is_equal, op1=ALU.mult, accum_out=rank[h][:, j:j + 1])
                        i.then_inc(ranked, 1)
                        v.wait_ge(selected, m * HALF + HALF + 2)
                        v.wait_ge(ranked, m + 3)
                        v.wait_ge(sent, m + 1)
                        v.tensor_tensor(place[h][:], before[h][:], rank[h][:], ALU.add).then_inc(placed, 1)
                        v.wait_ge(placed, m + 3)

            @block.scalar
            def _(a):
                a.sem_inc(hiT_ready, 2)

                def turn(to, m, q):
                    a.wait_ge(flipped, m * 4 + q + 1)
                    a.activation(hiT[to][:, q * 2 * P:(q + 1) * 2 * P], ps_hiT[q % 2][:], ACT.Copy).then_inc(hiT_ready, 1)
                for q in range(4):
                    turn(0, 0, q)
                with a.Fori(0, LOOPS) as it:
                    for h in range(2):
                        m = it * 2 + h
                        a.wait_ge(ranked, m + 1)
                        a.dma_start(row_key[h][:], key_flat[bass.ds(m * HALF * P, HALF * P)].partition_broadcast(P)).then_inc(row_loaded[h], 16)
                        for j in range(HALF):
                            n = m * HALF + j
                            a.wait_ge(updated, n + 1 + HALF)
                            a.activation(count[j % 4][:], ps_count[:], ACT.Copy).then_inc(count_ready, 1)
                            if 3 <= j < 7:
                                turn(1 - h, m + 1, j - 3)
                        a.wait_ge(sent, m + 1)
                        a.activation(pay[h][:, :, 0], idx_i[:, bass.ds(m * HALF, HALF)], ACT.Copy)
                        a.activation(pay[h][:, :, 1], key[:, bass.ds(m * HALF, HALF)], ACT.Copy)
                        a.activation(pay[h][:, :, 2], lo[:, bass.ds(m * HALF, HALF)], ACT.Copy).then_inc(paid, 1)

            @block.tensor
            def _(t):
                t.matmul(ps_count[:], c["ident"][0:KEYS_HI, 0:KEYS_HI], start[:], start=True, stop=True, skip_group_check=True).then_inc(updated, HALF + 1)

                def flip(to, m, q):
                    t.wait_ge(hots, m * 4 + q + 1)
                    t.wait_ge(hiT_ready, m * 4 + q + 1)
                    for j in (2 * q, 2 * q + 1):
                        i = t.matmul(ps_hiT[q % 2][:, j % 2 * P:(j % 2 + 1) * P], hi_one[to][:, j, :], identb[:], start=True, stop=True)
                    i.then_inc(flipped, 1)
                for q in range(4):
                    flip(0, 0, q)
                with t.Fori(0, LOOPS) as it:
                    for h in range(2):
                        m = it * 2 + h
                        for j in range(HALF):
                            n = m * HALF + j
                            t.wait_ge(count_ready, n + 1)
                            t.matmul(ps_count[:], hi_one[h][:, j, :], lo_one[h][:, j, :], start=False, stop=True, skip_group_check=True).then_inc(updated, 1)
                            t.wait_ge(selected, n + 1)
                            t.wait_ge(hiT_ready, m * 4 + j // 2 + 3)
                            t.matmul(ps_at[j % 2][:], hiT[h][:, j * P:(j + 1) * P], count[j % 4][:], start=True, stop=True).then_inc(found, 1)
                            if 2 <= j < 6:
                                flip(1 - h, m + 1, j - 2)

            @block.gpsimd
            def _(e):
                last = e.to_reg(g.pos - 1)
                with e.Fori(0, LOOPS) as it:
                    for h in range(2):
                        m = it * 2 + h
                        e.wait_ge(placed, m + 3)
                        e.wait_ge(paid, m + 1)
                        e.sem_inc(issued, 1)
                        for j in range(HALF):
                            e.indirect_dma_start(out=sorted_rows, out_offset=bass.IndirectOffsetOnAxis(ap=place[h][:, j:j + 1], axis=0),
                                                 in_=pay[h][:, j, :], in_offset=None, bounds_check=last, oob_is_err=False).then_inc(scattered[h], 16)
                for h in range(2):
                    e.wait_ge(scattered[h], 16 * HALF * LOOPS)


def unpack(nc, c, g, sorted_rows, first, key_line, lo_line, idx, lo, item_block):
    C, T = g.chunks, g.chunk
    with Region(nc, g.name + "_unpack") as r:
        rows = [r.sb(f"rows{i}", [T, P, 4]) for i in range(2)]
        part = [r.sb(f"part{i}", [T, 3, P]) for i in range(2)]
        at = r.sb("at", [KEYS_HI, g.items])
        at_i = r.sb("at_i", [KEYS_HI, g.items], I32)
        counted = r.sb("counted_b", [KEYS_HI, P])
        ps = [r.ps(f"ps_part{i}", [P, 2, T]) for i in range(2)]
        ps_item = r.ps("ps_item", [P, 2, 512])
        loaded = [r.sem(f"rows_loaded{i}") for i in range(2)]
        lined = [r.sem(f"lined{i}") for i in range(2)]
        apart, turned, copied = r.sem("apart"), r.sem("parts_turned"), r.sem("copied")
        item, item_made, item_sum = r.sem("item"), r.sem("item_made"), r.sem("item_sum")
        half = g.items // 2
        with nc.Block() as block:
            @block.sync
            def _(s):
                for k in range(C):
                    if k >= 2:
                        s.wait_ge(apart, k - 1)
                    s.dma_start(rows[k % 2][:], sorted_rows[k * T * P:(k + 1) * T * P, :].rearrange("(t p) f -> t p f", p=P)).then_inc(loaded[k % 2], 16)
                    if k >= 1:
                        s.wait_ge(apart, k)
                        for i, line in enumerate((key_line, lo_line)):
                            s.dma_start(line[(k - 1) * T * P:k * T * P].rearrange("(t p) -> t p", p=P), part[(k - 1) % 2][:, i + 1, :]).then_inc(lined[(k - 1) % 2], 16)
                s.wait_ge(apart, C)
                for i, line in enumerate((key_line, lo_line)):
                    s.dma_start(line[(C - 1) * T * P:C * T * P].rearrange("(t p) -> t p", p=P), part[(C - 1) % 2][:, i + 1, :]).then_inc(lined[(C - 1) % 2], 16)
                s.wait_ge(lined[0], 32 * ((C + 1) // 2))
                s.wait_ge(lined[1], 32 * (C // 2))

            @block.vector
            def _(v):
                for k in range(C):
                    v.wait_ge(loaded[k % 2], 16 * (k // 2 + 1))
                    if k >= 2:
                        v.wait_ge(lined[k % 2], 32 * (k // 2))
                        v.wait_ge(turned, k - 1)
                    v.tensor_copy(part[k % 2][:], rows[k % 2][:, :, 0:3].rearrange("t p f -> t f p")).then_inc(apart, 1)
                v.wait_ge(item, 3)
                v.tensor_copy(at[:], at_i[:]).then_inc(item_made, 1)
                v.wait_ge(item_made, 1)
                v.tensor_scalar(at[:], at[:], first[:, 0:1], None, ALU.is_ge).then_inc(item_made, 1)
                v.wait_ge(item_sum, 1)
                v.tensor_copy(item_block[:].rearrange("p (a b) -> p a b", a=2), ps_item[0:1, :, 0:half]).then_inc(item_made, 1)
                v.wait_ge(item_made, 3)

            @block.gpsimd
            def _(e):
                e.iota(at_i[:], pattern=[[STEP * P, g.items]], base=0, channel_multiplier=0).then_inc(item, 1)
                e.memset(counted[:], 1.0).then_inc(item, 1)
                e.wait_ge(item, 2)
                e.affine_select(out=counted[:], in_=counted[:], compare_op=ALU.is_gt, fill=0.0, base=0,
                                pattern=[[0, P]], channel_multiplier=1).then_inc(item, 1)

            @block.tensor
            def _(t):
                for k in range(C):
                    t.wait_ge(apart, k + 1)
                    if k >= 2:
                        t.wait_ge(copied, 2 * (k - 1))
                    t.transpose(ps[k % 2][:, 0, :], part[k % 2][:, 0, :], c["ident"][0:T, 0:T])
                    t.transpose(ps[k % 2][:, 1, :], part[k % 2][:, 2, :], c["ident"][0:T, 0:T]).then_inc(turned, 1)
                t.wait_ge(item_made, 2)
                for a in range(2):
                    i = t.matmul(ps_item[:, a, 0:half], counted[:], at[:, a * half:(a + 1) * half], start=True, stop=True)
                i.then_inc(item_sum, 1)

            @block.scalar
            def _(a):
                for k in range(C):
                    a.wait_ge(turned, k + 1)
                    a.activation(idx[:, k * T:(k + 1) * T], ps[k % 2][:, 0, :], ACT.Copy).then_inc(copied, 1)
                    a.activation(lo[:, k * T:(k + 1) * T], ps[k % 2][:, 1, :], ACT.Copy).then_inc(copied, 1)
                a.wait_ge(copied, 2 * C)


def attention_scores(nc, c, g, idx, lo_line, item_block, q_sb, k_rows, scores):
    LOOPS = g.items // (2 * H)
    with Region(nc, "score") as r:
        slot = [r.sb(f"slot{i}", [P, TH], I32) for i in range(2)]
        k_got = [r.sb(f"k_got{i}", [P, STEP * D]) for i in range(H)]
        hot = [r.sb(f"hot{i}", [P, TH * P]) for i in range(2)]
        prod = [r.sb(f"prod{i}", [P, STEP * D]) for i in range(2)]
        s_tile = [r.sb(f"s_tile{i}", [P, TH, HEADS]) for i in range(2)]
        s_line = [r.sb(f"s_line{i}", [P, P]) for i in range(2)]
        ps_q = [r.ps(f"ps_q{i}", [P, STEP * D]) for i in range(2)]
        ps_s = [r.ps(f"ps_s{i}", [P, P]) for i in range(2)]
        slotted, hot_ready, expanded, issued = r.sem("slotted"), r.sem("hot_ready"), r.sem("expanded"), r.sem("issued")
        got = [r.sem(f"got{i}") for i in range(H)]
        row_loaded = [r.sem(f"row_loaded{i}") for i in range(2)]
        multiplied, reduced, turned, lined = r.sem("multiplied"), r.sem("reduced"), r.sem("turned"), r.sem("lined")
        stored, line_free = r.sem("stored"), r.sem("line_free")
        out = scores.rearrange("t h p -> (t h) p")
        with nc.Block() as block:
            @block.sync
            def _(s):
                def load(to, m):
                    s.dma_start(hot[to][:], lo_line[bass.ds(m * TH * P, TH * P)].partition_broadcast(P)).then_inc(row_loaded[to], 16)

                def body(it, last=False):
                    for h in range(2):
                        m = it * 2 + h
                        if not (last and h):
                            s.wait_ge(expanded, (m + 1) * H)
                            load(1 - h, m + 1)
                        if h:
                            store(0, m - 1)
                    store(1, m)

                def store(h, m):
                    s.wait_ge(lined, m + 3)
                    s.dma_start(out[bass.ds(m * P, P), :], s_line[h][:]).then_inc(stored, 16)
                    s.wait_ge(stored, m * 16 + 16)
                    s.sem_inc(line_free, 1)
                s.sem_inc(line_free, 2)
                load(0, 0)
                with s.Fori(0, LOOPS - 1) as it:
                    body(it)
                body(LOOPS - 1, True)

            @block.scalar
            def _(a):
                def put_slot(h, m):
                    a.activation(slot[h][:], idx[:, bass.ds(m * TH, TH)], ACT.Copy).then_inc(slotted, 1)

                def body(it, last=False):
                    for h in range(2):
                        m = it * 2 + h
                        if not last:
                            a.wait_ge(multiplied, (m + 2) * H)
                            put_slot(h, m + 2)
                        a.wait_ge(turned, m + 3)
                        a.wait_ge(line_free, m + 1)
                        a.activation(s_line[h][:], ps_s[h][:], ACT.Copy).then_inc(lined, 1)
                a.sem_inc(lined, 2)
                put_slot(0, 0)
                put_slot(1, 1)
                with a.Fori(0, LOOPS - 1) as it:
                    body(it)
                body(LOOPS - 1, True)

            @block.gpsimd
            def _(e):
                with e.Fori(0, LOOPS) as it:
                    for k in range(2 * H):
                        n, h, i = it * 2 * H + k, k // H, k % H
                        if i == 0:
                            e.wait_ge(slotted, it * 2 + h + 1)
                        e.wait_ge(multiplied, n + 1)
                        e.sem_inc(issued, 1)
                        for j in range(STEP):
                            e.indirect_dma_start(out=k_got[i][:, j * D:(j + 1) * D], out_offset=None, in_=k_rows,
                                                 in_offset=bass.IndirectOffsetOnAxis(ap=slot[h][:, i * STEP + j:i * STEP + j + 1], axis=0)).then_inc(got[i], 16)

            @block.tensor
            def _(t):
                def turn(h, m):
                    t.wait_ge(reduced, (m + 1) * H)
                    t.wait_ge(lined, m + 1)
                    t.transpose(ps_s[h][:], s_tile[h][:].rearrange("p t h -> p (t h)"), c["ident"][:]).then_inc(turned, 1)
                t.sem_inc(expanded, H)
                t.sem_inc(turned, 2)
                with t.Fori(0, LOOPS) as it:
                    for k in range(2 * H):
                        n, h, i = it * 2 * H + k, k // H, k % H
                        b = t.value_load(item_block[:, bass.ds(n, 1)], min_val=0, max_val=BLOCKS - 1)
                        if i == 0:
                            t.wait_ge(hot_ready, it * 2 + h + 1)
                        t.wait_ge(multiplied, n - 1 + H)
                        for j in range(STEP):
                            e = (i * STEP + j) * P
                            p = t.matmul(ps_q[k % 2][:, j * D:(j + 1) * D], hot[h][:, e:e + P], q_sb[:, b, :], start=True, stop=True)
                        p.then_inc(expanded, 1)
                        if k == H + 2:
                            turn(0, it * 2)
                    turn(1, it * 2 + 1)

            @block.vector
            def _(v):
                def compare(h, m):
                    v.wait_ge(row_loaded[h], (m - h) * 8 + 16)
                    v.tensor_scalar(hot[h][:], hot[h][:], c["col"][:, 0:1], None, ALU.is_equal).then_inc(hot_ready, 1)

                def reduce(n, k):
                    v.wait_ge(multiplied, n + 1 + H)
                    i = k % H
                    v.tensor_reduce(s_tile[k // H][:, i * STEP:(i + 1) * STEP, :], prod[k % 2][:].rearrange("p (t d h) -> p t h d", t=STEP, h=HEADS),
                                    AX.X, ALU.add).then_inc(reduced, 1)

                def body(it, last=False):
                    for k in range(2 * H):
                        n, m, i = it * 2 * H + k, it * 2 + k // H, k % H
                        v.wait_ge(got[i], m * 16 * STEP + 16 * STEP)
                        v.wait_ge(expanded, n + 1 + H)
                        if k > 1:
                            v.wait_ge(reduced, n - 1)
                        v.tensor_tensor(prod[k % 2][:], k_got[i][:], ps_q[k % 2][:], ALU.mult).then_inc(multiplied, 1)
                        if k:
                            if i == 1:
                                v.wait_ge(turned, m + 1)
                            reduce(n - 1, k - 1)
                        if i == H // 2 and not (last and k > H):
                            compare(1 - k // H, m + 1)
                    reduce(n, k)
                    v.wait_ge(reduced, n + 1)
                v.sem_inc(multiplied, H)
                compare(0, 0)
                with v.Fori(0, LOOPS - 1) as it:
                    body(it)
                body(LOOPS - 1, True)


def segment_softmax(nc, c, g, heads, scores, key_line, probs):
    R, W = g.chunk, g.chunks * P
    with Region(nc, g.name + "_softmax") as r:
        key = r.sb("key", [R, W + 2])
        cut = r.sb("cut", [R, W + 1])
        s = r.sb("s", [R, heads, W])
        f = r.sb("f", [R, heads, W])
        back = r.sb("back", [R, W])
        ends = r.sb("ends", [P, 2, P])
        over = r.sb("over", [P, P + 1])
        carry = r.sb("carry", [R, heads])
        ps_ends = r.ps("ps_ends", [P, 2, P])
        ps_carry = r.ps("ps_carry", [P, P])
        loaded, bare, done, turned, sent, stored = r.sem("loaded"), r.sem("bare"), r.sem("done"), r.sem("turned"), r.sem("sent"), r.sem("stored")
        ready, raised = r.sem("ready"), r.sem("raised")
        with nc.Block() as block:
            @block.sync
            def _(q):
                q.wait_ge(bare, 2)
                line = key_line.rearrange("(p w) -> p w", w=W)
                q.dma_start(key[:, 1:W + 1], line).then_inc(loaded, 16)
                q.dma_start(key[1:R, 0:1], line[0:R - 1, W - 1:W], allow_slow_non_contiguous=True).then_inc(loaded, 16)
                q.dma_start(key[0:R - 1, W + 1:W + 2], line[1:R, 0:1], allow_slow_non_contiguous=True).then_inc(loaded, 16)
                for h in range(heads):
                    q.dma_start(s[:, h, :].rearrange("r (t p) -> r t p", p=P), scores.rearrange("(r t) h p -> h r t p", r=R)[h]).then_inc(loaded, 16)
                for h in range(heads):
                    q.wait_ge(raised, h + 1)
                    q.dma_start(probs.rearrange("(r t) h p -> h r t p", r=R)[h], f[:, h, :].rearrange("r (t p) -> r t p", p=P)).then_inc(stored, 16)
                q.wait_ge(stored, 16 * heads)

            @block.tensor
            def _(t):
                for i in range(2):
                    t.wait_ge(sent, 2 * i + 1)
                    t.transpose(ps_ends[:, 0, :], ends[:, 0, :], c["ident"][:])
                    t.transpose(ps_ends[:, 1, :], ends[:, 1, :], c["ident"][:]).then_inc(turned, 1)
                    t.wait_ge(sent, 2 * i + 2)
                    t.transpose(ps_carry[:], over[:, 0:P] if i == 0 else over[:, 1:P + 1], c["ident"][:]).then_inc(turned, 1)

            @block.scalar
            def _(a):
                for h in range(heads):
                    a.wait_ge(ready, h + 1)
                    a.activation(f[:, h, :], f[:, h, :], ACT.Exp).then_inc(raised, 1)

            @block.vector
            def _(v):
                v.memset(key[:, 0:1], -2.0).then_inc(bare, 1)
                v.memset(key[:, W + 1:W + 2], -2.0).then_inc(bare, 1)
                ch = Chain(v, done)
                ch.inc(v.memset(ends[:], 0.0))
                ch.inc(v.memset(over[:], LOWEST))
                v.wait_ge(loaded, 16 * (3 + heads))
                ch.inc(v.tensor_tensor(cut[:], key[:, 0:W + 1], key[:, 1:W + 2], ALU.is_equal))
                ch.wait()
                ch.inc(v.tensor_scalar(cut[:], cut[:], -1.0, -LOWEST, ALU.add, ALU.mult))
                ch.wait()
                for i in range(2):
                    fwd = i == 0
                    edge = cut[:, 0:W] if fwd else cut[:, 1:W + 1][:, ::-1]

                    def run(ap):
                        return ap if fwd else ap[:, ::-1]
                    for h in range(heads):
                        src = s[:, h, :] if fwd else f[:, h, :]
                        ch.inc(v.tensor_tensor_scan(run(back[:]), edge, run(src), LOWEST, ALU.add, ALU.max))
                        ch.wait()
                        ch.inc(v.tensor_copy(ends[0:R, 0, h:h + 1], back[:, W - 1:W] if fwd else back[:, 0:1]))
                        ch.wait()
                    ch.inc(v.tensor_reduce(carry[:, 0:1], edge, AX.X, ALU.min))
                    ch.wait()
                    v.tensor_copy(ends[0:R, 1, 0:heads], carry[:, 0:1].to_broadcast([R, heads])).then_inc(sent, 1)
                    v.wait_ge(turned, 2 * i + 1)
                    ch.inc(v.tensor_copy(back[0:heads, 0:R], ps_ends[0:heads, 1, 0:R]))
                    ch.inc(v.memset(over[:], LOWEST))
                    ch.wait()
                    to = over[0:heads, 1:R + 1] if fwd else over[0:heads, 0:R][:, ::-1]
                    v.tensor_tensor_scan(to, run(back[0:heads, 0:R]), run(ps_ends[0:heads, 0, 0:R]), LOWEST, ALU.add, ALU.max).then_inc(sent, 1)
                    v.wait_ge(turned, 2 * i + 2)
                    ch.inc(v.tensor_copy(carry[:], ps_carry[0:R, 0:heads]))
                    ch.wait()
                    for h in range(heads):
                        src = s[:, h, :] if fwd else f[:, h, :]
                        ch.inc(v.tensor_tensor_scan(run(f[:, h, :]), edge, run(src), carry[:, h:h + 1], ALU.add, ALU.max))
                    ch.wait()
                for h in range(heads):
                    v.tensor_tensor(f[:, h, :], s[:, h, :], f[:, h, :], ALU.subtract).then_inc(ready, 1)


def attention_sum(nc, c, g, idx, lo, item_block, v_rows, probs, acc):
    LOOPS = g.items // (2 * H)
    A = D + HEADS
    RING = 4
    with Region(nc, "sum") as r:
        slot = [r.sb(f"slot{i}", [P, TH], I32) for i in range(2)]
        v_got = [r.sb(f"v_got{i}", [P, STEP * D]) for i in range(H)]
        p_line = [r.sb(f"p_line{i}", [P, P]) for i in range(2)]
        p_tile = [r.sb(f"p_tile{i}", [P, TH, HEADS]) for i in range(2)]
        hot = [r.sb(f"hot{i}", [P, STEP, P]) for i in range(RING)]
        w = [r.sb(f"w{i}", [P, STEP, A]) for i in range(RING)]
        ps_p = [r.ps(f"ps_p{i}", [P, TH, HEADS]) for i in range(2)]
        ps_a = [r.ps(f"ps_a{i}", [P, A]) for i in range(RING)]
        slotted, turned, tiled = r.sem("slotted"), r.sem("turned"), r.sem("tiled")
        p_loaded = [r.sem(f"p_loaded{i}") for i in range(2)]
        got = [r.sem(f"got{i}") for i in range(H)]
        weighted, summed, added, issued, beside = r.sem("weighted"), r.sem("summed"), r.sem("added"), r.sem("issued"), r.sem("beside")
        src = probs.rearrange("t h p -> (t h) p")
        with nc.Block() as block:
            @block.sync
            def _(s):
                with s.Fori(0, LOOPS) as it:
                    for h in range(2):
                        m = it * 2 + h
                        s.wait_ge(turned, m + 1)
                        s.dma_start(p_line[h][:], src[bass.ds(m * P, P), :]).then_inc(p_loaded[h], 16)

            @block.scalar
            def _(a):
                def put_slot(h, m):
                    a.activation(slot[h][:], idx[:, bass.ds(m * TH, TH)], ACT.Copy).then_inc(slotted, 1)

                def put_p(h, m):
                    a.wait_ge(turned, m + 3)
                    a.activation(p_tile[h][:], ps_p[h][:], ACT.Copy).then_inc(tiled, 1)

                def body(it, last=False):
                    for k in range(2 * H):
                        n, h, i, m = it * 2 * H + k, k // H, k % H, it * 2 + k // H
                        if i == 1 and not (last and h):
                            a.wait_ge(weighted, (m + 1) * H)
                            put_p(1 - h, m + 1)
                        if i == 1 and not (last and h):
                            put_slot(1 - h, m + 1)
                        if i == 0:
                            a.wait_ge(tiled, m + 3)
                        a.wait_ge(summed, n + 1)
                        a.activation(w[k % RING][:, :, D:A], p_tile[h][:, i * STEP:(i + 1) * STEP, :], ACT.Copy).then_inc(beside, 1)
                a.sem_inc(tiled, 2)
                put_slot(0, 0)
                put_p(0, 0)
                with a.Fori(0, LOOPS - 1) as it:
                    body(it)
                body(LOOPS - 1, True)

            @block.gpsimd
            def _(e):
                with e.Fori(0, LOOPS) as it:
                    for k in range(2 * H):
                        n, h, i = it * 2 * H + k, k // H, k % H
                        if i == 0:
                            e.wait_ge(slotted, it * 2 + h + 1)
                        e.wait_ge(weighted, n + 1)
                        e.sem_inc(issued, 1)
                        for j in range(STEP):
                            e.indirect_dma_start(out=v_got[i][:, j * D:(j + 1) * D], out_offset=None, in_=v_rows,
                                                 in_offset=bass.IndirectOffsetOnAxis(ap=slot[h][:, i * STEP + j:i * STEP + j + 1], axis=0)).then_inc(got[i], 16)

            @block.tensor
            def _(t):
                def turn(h, m):
                    t.wait_ge(p_loaded[h], (m - h) * 8 + 16)
                    t.wait_ge(tiled, m + 1)
                    t.transpose(ps_p[h][:].rearrange("p t h -> p (t h)"), p_line[h][:], c["ident"][:]).then_inc(turned, 1)

                def body(it, last=False):
                    for k in range(2 * H):
                        n = it * 2 * H + k
                        t.wait_ge(weighted, n + 1 + H)
                        t.wait_ge(beside, n + 1)
                        t.wait_ge(added, n + 1)
                        for j in range(STEP):
                            i = t.matmul(ps_a[k % RING][:], hot[k % RING][:, j, :], w[k % RING][:, j, :], start=j == 0, stop=j == STEP - 1)
                        i.then_inc(summed, 1)
                        if k % H == 0 and not (last and k):
                            turn(1 - k // H, it * 2 + k // H + 1)
                t.sem_inc(summed, RING)
                t.sem_inc(turned, 2)
                turn(0, 0)
                with t.Fori(0, LOOPS - 1) as it:
                    body(it)
                body(LOOPS - 1, True)

            @block.vector
            def _(v):
                def add(n, k):
                    b = v.value_load(item_block[:, bass.ds(n, 1)], min_val=0, max_val=BLOCKS - 1)
                    v.wait_ge(summed, n + 1 + RING)
                    v.wait_ge(added, n + RING)
                    v.tensor_tensor(acc[:, b, :], acc[:, b, :], ps_a[k % RING][:], ALU.add).then_inc(added, 1)
                v.sem_inc(weighted, H)
                v.memset(acc[:], 0.0).then_inc(added, 1)
                v.wait_ge(added, 1)
                v.sem_inc(added, RING - 1)
                with v.Fori(0, LOOPS) as it:
                    for k in range(2 * H):
                        n, m, i = it * 2 * H + k, it * 2 + k // H, k % H
                        v.wait_ge(summed, n + 1)
                        v.tensor_tensor(hot[k % RING][:], c["iota"][:].unsqueeze(1).to_broadcast([P, STEP, P]),
                                        lo[:, bass.ds(n * STEP, STEP)].unsqueeze(2).to_broadcast([P, STEP, P]), ALU.is_equal)
                        v.wait_ge(got[i], m * 16 * STEP + 16 * STEP)
                        if i == 0:
                            v.wait_ge(tiled, m + 3)
                        v.tensor_tensor(w[k % RING][:, :, 0:D].rearrange("p t (d h) -> p t d h", h=HEADS), v_got[i][:].rearrange("p (t d h) -> p t d h", t=STEP, h=HEADS),
                                        p_tile[k // H][:, i * STEP:(i + 1) * STEP, :].unsqueeze(2).to_broadcast([P, STEP, HD, HEADS]), ALU.mult).then_inc(weighted, 1)
                        if k:
                            add(n - 1, k - 1)
                    add(n, k)
                v.wait_ge(added, g.items + RING)


def attention_out(nc, c, acc, w_out, b_out, x_sb):
    A = D + HEADS
    AHEAD = 4
    with Region(nc, "out") as r:
        W = r.sb("W", [P, 2, D])
        brow = r.sb("brow", [P, D])
        inv = r.sb("inv", [P, NB, HEADS])
        stage = r.sb("stage", [P, AHEAD + 1, D])
        yT = r.sb("yT", [P, 2, D])
        psT = [r.ps(f"psT{i}", [P, D]) for i in range(2)]
        ps_y = [r.ps(f"ps_y{i}", [P, D]) for i in range(2)]
        loaded, inverse, staged, turned = r.sem("loaded"), r.sem("inverse"), r.sem("staged"), r.sem("turned")
        yT_ready, multiplied, added = r.sem("yT_ready"), r.sem("multiplied"), r.sem("added")
        with nc.Block() as block:
            @block.sync
            def _(s):
                s.dma_start(W[:], w_out.rearrange("(c p) n -> p c n", p=P)).then_inc(loaded, 16)
                s.dma_start(brow[:], b_out.partition_broadcast(P)).then_inc(loaded, 16)
                s.wait_ge(loaded, 32)

            @block.vector
            def _(v):
                ch = Chain(v, inverse)
                ch.inc(v.tensor_scalar(inv[:], acc[:, :, D:A], 1e-30, None, ALU.max))
                ch.wait()
                ch.inc(v.reciprocal(inv[:], inv[:]))
                v.wait_ge(loaded, 32)
                ch.inc(v.tensor_tensor(x_sb[:], x_sb[:], brow[:].unsqueeze(1).to_broadcast([P, NB, D]), ALU.add))
                ch.wait()
                v.sem_inc(added, 2)
                def put_stage(n, k):
                    v.wait_ge(turned, n + 2 - AHEAD if k >= AHEAD else it * U + 2)
                    v.tensor_tensor(stage[:, k % (AHEAD + 1), :].rearrange("p (d h) -> p d h", h=HEADS), acc[:, n, 0:D].rearrange("p (d h) -> p d h", h=HEADS),
                                    inv[:, n, :].unsqueeze(1).to_broadcast([P, HD, HEADS]), ALU.mult).then_inc(staged, 1)
                with v.Fori(0, NB // U) as it:
                    for k in range(AHEAD):
                        put_stage(it * U + k, k)
                    for k in range(U):
                        n = it * U + k
                        if k + AHEAD < U:
                            put_stage(n + AHEAD, k + AHEAD)
                        v.wait_ge(multiplied, n + 3)
                        v.tensor_tensor(x_sb[:, n, :], x_sb[:, n, :], ps_y[k % 2][:], ALU.add).then_inc(added, 1)

            @block.tensor
            def _(t):
                t.sem_inc(turned, 2)
                t.sem_inc(multiplied, 2)
                t.wait_ge(loaded, 32)
                with t.Fori(0, NB // U) as it:
                    def turn(n, k):
                        t.wait_ge(staged, n + 1)
                        t.wait_ge(yT_ready, n + 1)
                        t.transpose(psT[k % 2][:, 0:P], stage[:, k % (AHEAD + 1), 0:P], c["ident"][:])
                        t.transpose(psT[k % 2][:, P:D], stage[:, k % (AHEAD + 1), P:D], c["ident"][:]).then_inc(turned, 1)
                    turn(it * U, 0)
                    for k in range(U):
                        n = it * U + k
                        if k + 1 < U:
                            turn(n + 1, k + 1)
                        t.wait_ge(yT_ready, n + 3)
                        t.wait_ge(added, n + 1)
                        for h in range(2):
                            m = t.matmul(ps_y[k % 2][:], yT[:, k % 2, h * P:(h + 1) * P], W[:, h, :], start=h == 0, stop=h == 1)
                        m.then_inc(multiplied, 1)

            @block.scalar
            def _(a):
                a.sem_inc(yT_ready, 2)
                with a.Fori(0, NB // U) as it:
                    for k in range(U):
                        n = it * U + k
                        a.wait_ge(turned, n + 3)
                        a.wait_ge(multiplied, n + 1)
                        a.activation(yT[:, k % 2, :], psT[k % 2][:], ACT.Copy).then_inc(yT_ready, 1)


def gat_rows(nc, c, xc, rstd, w_gat, att_src, att_dst, xT_all, table, a_dst):
    F = GH * EX
    with Region(nc, "gat_rows") as r:
        W = r.sb("W", [P, 2, F])
        att = r.sb("att", [P, 2, F])
        rows = r.sb("rows", [P, NB, GROW])
        prod = r.sb("prod", [P, 2, NB, F])
        stage = r.sb("stage", [P, 2, D])
        xT = r.sb("xT", [P, 2, D])
        psT = [r.ps(f"psT{i}", [P, D]) for i in range(2)]
        ps_h = [r.ps(f"ps_h{i}", [P, F]) for i in range(2)]
        loaded, staged, turned, xT_ready = r.sem("loaded"), r.sem("staged"), r.sem("turned"), r.sem("xT_ready")
        kept, multiplied, taken, scored, stored = r.sem("kept"), r.sem("multiplied"), r.sem("taken"), r.sem("scored"), r.sem("stored")
        with nc.Block() as block:
            @block.sync
            def _(s):
                s.dma_start(W[:], w_gat.rearrange("(c p) n -> p c n", p=P)).then_inc(loaded, 16)
                s.dma_start(att[:, 0, :], att_src.rearrange("h e -> (h e)").partition_broadcast(P)).then_inc(loaded, 16)
                s.dma_start(att[:, 1, :], att_dst.rearrange("h e -> (h e)").partition_broadcast(P)).then_inc(loaded, 16)
                s.wait_ge(scored, 4)
                s.dma_start(table.rearrange("(b p) f -> p b f", p=P), rows[:]).then_inc(stored, 16)
                s.wait_ge(stored, 16)

            @block.scalar
            def _(a):
                def put_stage(n, k):
                    a.wait_ge(turned, n + 1)
                    a.activation(stage[:, k % 2, :], xc[:, n, :], ACT.Copy, scale=rstd[:, bass.ds(n, 1)]).then_inc(staged, 1)
                a.sem_inc(xT_ready, 2)
                with a.Fori(0, NB // U) as it:
                    put_stage(it * U, 0)
                    for k in range(U):
                        n = it * U + k
                        if k + 1 < U:
                            put_stage(n + 1, k + 1)
                        a.wait_ge(turned, n + 3)
                        a.wait_ge(multiplied, n + 1)
                        a.wait_ge(kept, n + 1)
                        a.activation(xT[:, k % 2, :], psT[k % 2][:], ACT.Copy).then_inc(xT_ready, 1)

            @block.tensor
            def _(t):
                t.sem_inc(turned, 2)
                t.sem_inc(multiplied, 2)
                t.wait_ge(loaded, 48)
                with t.Fori(0, NB // U) as it:
                    def turn(n, k):
                        t.wait_ge(staged, n + 1)
                        t.wait_ge(xT_ready, n + 1)
                        t.transpose(psT[k % 2][:, 0:P], stage[:, k % 2, 0:P], c["ident"][:])
                        t.transpose(psT[k % 2][:, P:D], stage[:, k % 2, P:D], c["ident"][:]).then_inc(turned, 1)
                    turn(it * U, 0)
                    for k in range(U):
                        n = it * U + k
                        if k + 1 < U:
                            turn(n + 1, k + 1)
                        t.wait_ge(xT_ready, n + 3)
                        t.wait_ge(taken, n + 1)
                        for h in range(2):
                            m = t.matmul(ps_h[k % 2][:], xT[:, k % 2, h * P:(h + 1) * P], W[:, h, :], start=h == 0, stop=h == 1)
                        m.then_inc(multiplied, 1)

            @block.vector
            def _(v):
                v.sem_inc(kept, 2)
                v.sem_inc(taken, 2)
                with v.Fori(0, NB // U) as it:
                    for k in range(U):
                        n = it * U + k
                        v.wait_ge(xT_ready, n + 3)
                        v.tensor_copy(xT_all[:, :, bass.ds(n * P, P)], xT[:, k % 2, :].rearrange("p (c n) -> p c n", c=2)).then_inc(kept, 1)
                        v.wait_ge(multiplied, n + 3)
                        v.tensor_copy(rows[:, n, 0:F], ps_h[k % 2][:]).then_inc(taken, 1)
                v.wait_ge(taken, NB + 2)
                for i in range(2):
                    v.tensor_tensor(prod[:, i], rows[:, :, 0:F], att[:, i, :].unsqueeze(1).to_broadcast([P, NB, F]), ALU.mult).then_inc(scored, 1)
                v.wait_ge(scored, 2)
                for i, to in enumerate((rows[:, :, F:GROW], a_dst[:])):
                    v.tensor_reduce(to, prod[:, i].rearrange("p b (h e) -> p b h e", e=EX), AX.X, ALU.add).then_inc(scored, 1)
                v.wait_ge(scored, 4)


def gat_scores_and_experts(nc, c, g, idx, lo_line, item_block, table, a_dst, kept_rows, scores, xT_all, w1, b1, w2, b2, y):
    F = GH * EX
    FC = FF // P
    L = GT * GH
    LOOPS = g.items // (2 * GI)
    with Region(nc, "gat_score") as r:
        slot = [r.sb(f"slot{i}", [P, GT], I32) for i in range(2)]
        rows = [r.sb(f"rows{i}", [P, GT, GROW]) for i in range(2)]
        hot = [r.sb(f"hot{i}", [P, GT * P]) for i in range(2)]
        e_sum = r.sb("e_sum", [P, 2, GT, GH])
        s_tile = [r.sb(f"s_tile{i}", [P, GT, GH]) for i in range(2)]
        s_line = [r.sb(f"s_line{i}", [L, P]) for i in range(2)]
        W1 = r.sb("W1", [P, EX, 2, FF])
        W2 = r.sb("W2", [P, EX, FC, D])
        B1 = r.sb("B1", [P, EX, FC])
        B2 = r.sb("B2", [P, EX, D])
        hid = [r.sb(f"hid{i}", [P, FC, P]) for i in range(2)]
        y_sb = [r.sb(f"y_sb{i}", [P, EX, D]) for i in range(2)]
        ps_d = [r.ps(f"ps_d{i}", [P, GT, GH]) for i in range(2)]
        ps_s = r.ps("ps_s", [L, P])
        ps1 = [r.ps(f"ps1_{i}", [P, FC, P]) for i in range(2)]
        ps2 = [r.ps(f"ps2_{i}", [P, D]) for i in range(2)]
        clamped, slotted, hot_ready, expanded = r.sem("clamped"), r.sem("slotted"), r.sem("hot_ready"), r.sem("expanded")
        got, row_loaded, kept, stored, y_stored = ([r.sem(f"{n}{i}") for i in range(2)] for n in ("got", "row_loaded", "kept", "stored", "y_stored"))
        summed, leaked, turned, lined, issued = (r.sem(n) for n in ("summed", "leaked", "turned", "lined", "issued"))
        rows_free, line_free, y_free = r.sem("rows_free"), r.sem("line_free"), r.sem("y_free")
        w_loaded, first, active, second, added = (r.sem(n) for n in ("w_loaded", "first", "active", "second", "added"))
        out = scores.rearrange("t h p -> (t h) p")
        with nc.Block() as block:
            @block.sync
            def _(s):
                for e in range(EX):
                    s.dma_start(W1[:, e], w1[e].rearrange("(c p) f -> p c f", p=P)).then_inc(w_loaded, 16)
                    s.dma_start(W2[:, e], w2[e].rearrange("(c p) f -> p c f", p=P)).then_inc(w_loaded, 16)
                    s.dma_start(B1[:, e, :], b1[e].rearrange("(c p) -> p c", p=P), allow_slow_non_contiguous=True).then_inc(w_loaded, 16)
                    s.dma_start(B2[:, e, :], b2[e].partition_broadcast(P)).then_inc(w_loaded, 16)
                for free in (rows_free, line_free, y_free):
                    s.sem_inc(free, 2)

                def load(h, m):
                    s.dma_start(hot[h][:], lo_line[bass.ds(m * GT * P, GT * P)].partition_broadcast(P)).then_inc(row_loaded[h], 16)

                def body(it, last=False):
                    for h in range(2):
                        m = it * 2 + h
                        if not (last and h):
                            s.wait_ge(expanded, m + 1)
                            load(1 - h, m + 1)
                        s.wait_ge(got[h], it * (16 * GT) + 16 * GT)
                        s.dma_start(kept_rows[bass.ds(m * P, P), :], rows[h][:].rearrange("p t f -> p (t f)")).then_inc(kept[h], 16)
                        s.wait_ge(lined, m + 2)
                        s.dma_start(out[bass.ds(m * L, L), :], s_line[h][:]).then_inc(stored[h], 16)
                        s.wait_ge(added, (m + 1) * EX + 2)
                        s.dma_start(y[bass.ds(m * P, P), :], y_sb[h][:].rearrange("p e d -> p (e d)")).then_inc(y_stored[h], 16)
                        for done, free in ((kept, rows_free), (stored, line_free), (y_stored, y_free)):
                            s.wait_ge(done[h], it * 16 + 16)
                            s.sem_inc(free, 1)
                load(0, 0)
                with s.Fori(0, LOOPS - 1) as it:
                    body(it)
                body(LOOPS - 1, True)

            @block.scalar
            def _(a):
                def put_slot(h, m):
                    a.activation(slot[h][:], idx[:, bass.ds(m * GT, GT)], ACT.Copy).then_inc(slotted, 1)

                def body(it, last=False):
                    for h in range(2):
                        m = it * 2 + h
                        for e in range(EX):
                            q = m * EX + e
                            a.wait_ge(first, q + 1)
                            a.wait_ge(second, q + 1)
                            for f in range(FC):
                                i = a.activation(hid[e % 2][:, f, :], ps1[e % 2][:, f, :], ACT.Gelu, bias=B1[:, e, f:f + 1])
                            i.then_inc(active, 1)
                        if not last:
                            a.wait_ge(summed, m + 3)
                            put_slot(h, m + 2)
                        a.wait_ge(turned, m + 3)
                        a.wait_ge(line_free, m + 1)
                        a.activation(s_line[h][:], ps_s[:], ACT.Copy).then_inc(lined, 1)
                a.wait_ge(clamped, 1)
                a.sem_inc(lined, 1)
                a.sem_inc(active, 2)
                put_slot(0, 0)
                put_slot(1, 1)
                a.wait_ge(w_loaded, 64 * EX)
                with a.Fori(0, LOOPS - 1) as it:
                    body(it)
                body(LOOPS - 1, True)

            @block.gpsimd
            def _(e):
                with e.Fori(0, LOOPS) as it:
                    for h in range(2):
                        m = it * 2 + h
                        e.wait_ge(rows_free, m + 1)
                        e.wait_ge(summed, m + 1)
                        e.wait_ge(slotted, m + 1)
                        e.sem_inc(issued, 1)
                        for j in range(GT):
                            e.indirect_dma_start(out=rows[h][:, j, :], out_offset=None, in_=table,
                                                 in_offset=bass.IndirectOffsetOnAxis(ap=slot[h][:, j:j + 1], axis=0)).then_inc(got[h], 16)

            @block.tensor
            def _(t):
                t.sem_inc(expanded, 1)
                t.sem_inc(second, 2)
                t.sem_inc(turned, 2)
                t.wait_ge(w_loaded, 64 * EX)
                with t.Fori(0, LOOPS) as it:
                    for h in range(2):
                        m = it * 2 + h

                        def up(e):
                            t.wait_ge(active, m * EX + e + 1)
                            for f in range(FC):
                                for k in range(2):
                                    i = t.matmul(ps1[e % 2][:, f, :], W1[:, e, k, f * P:(f + 1) * P], xT_all[:, k, bass.ds(m * P, P)], start=k == 0, stop=k == 1)
                            i.then_inc(first, 1)

                        def down(e):
                            t.wait_ge(active, m * EX + e + 3)
                            t.wait_ge(added, m * EX + e + 1)
                            for f in range(FC):
                                i = t.matmul(ps2[e % 2][:], hid[e % 2][:, f, :], W2[:, e, f, :], start=f == 0, stop=f == FC - 1)
                            i.then_inc(second, 1)
                        up(0)
                        up(1)
                        t.wait_ge(hot_ready, m + 1)
                        t.wait_ge(summed, m + 1)
                        for k in range(GI):
                            if k % 4 == 0:
                                blocks = item_blocks(nc, PE, item_block, m * GI + k, 4)
                            for j in range(k * STEP, (k + 1) * STEP):
                                i = t.matmul(ps_d[h][:, j, :], hot[h][:, j * P:(j + 1) * P], a_dst[:, blocks[k % 4], :], start=True, stop=True)
                        i.then_inc(expanded, 1)
                        for e in range(EX - 1):
                            down(e)
                            if e + 2 < EX:
                                up(e + 2)
                        t.wait_ge(leaked, m + 1)
                        t.wait_ge(lined, m + 1)
                        t.transpose(ps_s[:], s_tile[h][:].rearrange("p t h -> p (t h)"), c["ident"][:]).then_inc(turned, 1)
                        down(EX - 1)

            @block.vector
            def _(v):
                v.tensor_scalar(idx[:], idx[:], N - 1, None, ALU.min).then_inc(clamped, 1)
                v.sem_inc(summed, 2)
                v.sem_inc(added, 2)
                v.wait_ge(w_loaded, 64 * EX)
                with v.Fori(0, LOOPS) as it:
                    for h in range(2):
                        m = it * 2 + h
                        v.wait_ge(row_loaded[h], it * 16 + 16)
                        v.tensor_scalar(hot[h][:], hot[h][:], c["col"][:, 0:1], None, ALU.is_equal).then_inc(hot_ready, 1)
                        v.wait_ge(y_free, m + 1)

                        def bias(e):
                            v.wait_ge(second, m * EX + e + 3)
                            v.tensor_tensor(y_sb[h][:, e, :], ps2[e % 2][:], B2[:, e, :], ALU.add).then_inc(added, 1)
                        bias(0)
                        bias(1)
                        v.wait_ge(got[h], it * (16 * GT) + 16 * GT)
                        v.wait_ge(expanded, m + 2)
                        v.tensor_tensor(e_sum[:, h], rows[h][:, :, F:GROW], ps_d[h][:], ALU.add).then_inc(summed, 1)
                        v.wait_ge(summed, m + 3)
                        v.wait_ge(turned, m + 1)
                        v.scalar_tensor_tensor(out=s_tile[h][:], in0=e_sum[:, h], scalar=0.2, in1=e_sum[:, h],
                                               op0=ALU.mult, op1=ALU.max).then_inc(leaked, 1)
                        bias(2)
                        bias(3)


def gat_sum(nc, c, g, lo, item_block, kept_rows, probs, acc):
    F = GH * EX
    LOOPS = g.items // (2 * GI)
    ROOM = 64
    PARTS = 3
    L = GT * GH
    with Region(nc, "gat_sum") as r:
        zero = r.sb("zero", [P, 512])
        p_line = [r.sb(f"p_line{i}", [L, P]) for i in range(2)]
        iota4 = r.sb("iota4", [P, P, 4], BF16)
        lo_b = r.sb("lo_b", [P, g.slots], BF16)
        hot = [r.sb(f"hot{i}", [P, GT // 4, P, 4], BF16) for i in range(2)]
        rows = [r.sb(f"rows{i}", [P, GT, GROW]) for i in range(2)]
        w = [r.sb(f"w{i}", [P, GT, GROW]) for i in range(2)]
        left = [r.sb(f"left{i}", [P, GT, GROW]) for i in range(2)]
        part = [r.sb(f"part{i}", [P, GT, PARTS, GROW], BF16) for i in range(2)]
        ps_p = r.ps("ps_p", [P, GT, GH])
        ps_acc = r.ps("ps_acc", [P, 7 * (512 // ROOM), ROOM])
        blank, narrowed, turned, beside, weighted, halved, lessened, parted, summed, taken, passed = (
            r.sem(n) for n in ("blank", "narrowed", "turned", "beside", "weighted", "halved", "lessened", "parted", "summed", "taken", "passed"))
        p_loaded = [r.sem(f"p_loaded{i}") for i in range(2)]
        row_loaded = [r.sem(f"row_loaded{i}") for i in range(2)]
        src = probs.rearrange("t h p -> (t h) p")
        with nc.Block() as block:
            @block.sync
            def _(s):
                with s.Fori(0, LOOPS) as it:
                    for h in range(2):
                        m = it * 2 + h
                        s.wait_ge(turned, m + 1)
                        s.dma_start(p_line[h][:], src[bass.ds(m * L, L), :]).then_inc(p_loaded[h], 16)
                        s.wait_ge(weighted, m + 1)
                        s.dma_start(rows[h][:].rearrange("p t f -> p (t f)"), kept_rows[bass.ds(m * P, P), :]).then_inc(row_loaded[h], 16)

            @block.gpsimd
            def _(e):
                e.memset(zero[:], 0.0).then_inc(blank, 1)
                with e.Fori(0, LOOPS) as it:
                    for h in range(2):
                        m = it * 2 + h
                        e.wait_ge(halved, m * 2 + 2)
                        e.wait_ge(lessened, m + 1)
                        e.sem_inc(passed, 1)
                        e.tensor_tensor(part[h][:, :, 2, :], left[h][:], part[h][:, :, 1, :], ALU.subtract).then_inc(parted, 1)

            @block.tensor
            def _(t):
                t.wait_ge(blank, 1)
                room = 512 // ROOM
                for i in range(7):
                    t.matmul(ps_acc[:, i * room:(i + 1) * room, :], zero[:, 0:P], zero[:], start=True, stop=True, skip_group_check=True)
                t.sem_inc(summed, 2)
                t.sem_inc(turned, 2)

                def turn(h, m):
                    t.wait_ge(p_loaded[h], (m - h) * 8 + 16)
                    t.wait_ge(weighted, m + 2)
                    t.wait_ge(beside, m + 2)
                    t.transpose(ps_p[:].rearrange("p t h -> p (t h)"), p_line[h][:], c["ident"][0:L, 0:L]).then_inc(turned, 1)

                def body(it, last=False):
                    for h in range(2):
                        m = it * 2 + h
                        blocks = item_blocks(nc, PE, item_block, m * GI, GI)
                        if not (last and h):
                            turn(1 - h, m + 1)
                        t.wait_ge(parted, m + 1)
                        for k in range(GI):
                            for j in range(k * STEP, (k + 1) * STEP):
                                i = t.matmul(ps_acc[:, blocks[k], 0:PARTS * GROW], hot[h][:, j // 4, :, j % 4], part[h][:, j].rearrange("p a f -> p (a f)"),
                                             start=False, stop=True, skip_group_check=True)
                        i.then_inc(summed, 1)
                turn(0, 0)
                with t.Fori(0, LOOPS - 1) as it:
                    body(it)
                body(LOOPS - 1, True)

            @block.scalar
            def _(a):
                a.sem_inc(beside, 2)
                with a.Fori(0, LOOPS) as it:
                    for h in range(2):
                        m = it * 2 + h
                        a.wait_ge(turned, m + 3)
                        a.wait_ge(summed, m + 1)
                        a.activation(w[h][:, :, F:GROW], ps_p[:], ACT.Copy).then_inc(beside, 1)
                        a.wait_ge(weighted, m + 3)
                        a.wait_ge(beside, m + 3)
                        a.activation(part[h][:, :, 0, :], w[h][:], ACT.Copy).then_inc(halved, 1)
                        a.wait_ge(lessened, m + 1)
                        a.activation(part[h][:, :, 1, :], left[h][:], ACT.Copy).then_inc(halved, 1)

            @block.vector
            def _(v):
                v.tensor_copy(iota4[:], c["iota"][:].unsqueeze(2).to_broadcast([P, P, 4]))
                v.tensor_copy(lo_b[:], lo[:]).then_inc(narrowed, 1)
                v.wait_ge(narrowed, 1)
                v.sem_inc(weighted, 2)
                with v.Fori(0, LOOPS) as it:
                    for h in range(2):
                        m = it * 2 + h
                        v.wait_ge(summed, m + 1)
                        v.wait_ge(beside, m + 3)
                        v.wait_ge(row_loaded[h], it * 16 + 16)
                        v.tensor_tensor(w[h][:, :, 0:F].rearrange("p t (h e) -> p t h e", e=EX), rows[h][:, :, 0:F].rearrange("p t (h e) -> p t h e", e=EX),
                                        ps_p[:].unsqueeze(3).to_broadcast([P, GT, GH, EX]), ALU.mult).then_inc(weighted, 1)
                        quad_one_hots(v, hot[h][:], iota4[:], lo_b[:, bass.ds(m * GT, GT)], GT)
                        v.wait_ge(halved, m * 2 + 1)
                        v.tensor_tensor(left[h][:], w[h][:], part[h][:, :, 0, :], ALU.subtract).then_inc(lessened, 1)
                v.wait_ge(summed, 2 * LOOPS + 2)
                v.tensor_copy(acc[:], ps_acc[:, 0:NB, 2 * GROW:3 * GROW]).then_inc(taken, 1)
                for i in (1, 0):
                    v.wait_ge(taken, 2 - i)
                    v.tensor_tensor(acc[:], acc[:], ps_acc[:, 0:NB, i * GROW:(i + 1) * GROW], ALU.add).then_inc(taken, 1)
                v.wait_ge(taken, PARTS)


def load_y(s, y, y_in, y_loaded, n, k):
    s.dma_start(y_in[k][:].rearrange("p e d -> p (e d)"), y[bass.ds(n * P, P), :]).then_inc(y_loaded[k], 16)


def route(nc, c, acc, b_gat, gamma, beta, gate, results, y_in, y_loaded):
    F = GH * EX
    with Region(nc, "route") as r:
        par = r.sb("par", [P, 3, F])
        inv = r.sb("inv", [P, NB, GH])
        y = r.sb("y", [P, NB, F])
        y2 = r.sb("y2", [P, NB, F])
        mean = r.sb("mean", [P, NB])
        var = r.sb("var", [P, NB])
        sc = r.sb("sc", [P, NB, EX])
        less = r.sb("less", [P, NB, EX, EX])
        same = r.sb("same", [P, NB, EX, EX])
        lower = r.sb("lower", [P, EX, EX])
        top = r.sb("top", [P, NB])
        loaded, done, low, vary, root, shifted, raised = (r.sem(n) for n in ("loaded", "done", "low", "vary", "root", "shifted", "raised"))
        with nc.Block() as block:
            @block.sync
            def _(s):
                for i, a in enumerate((b_gat, gamma, beta)):
                    s.dma_start(par[:, i, :], a.partition_broadcast(P)).then_inc(loaded, 16)
                for k in range(U):
                    load_y(s, results, y_in, y_loaded, k, k)
                s.wait_ge(loaded, 48)

            @block.gpsimd
            def _(e):
                e.memset(lower[:], 1.0).then_inc(low, 1)
                e.wait_ge(low, 1)
                e.affine_select(out=lower[:], in_=lower[:], compare_op=ALU.is_gt, fill=0.0, base=0,
                                pattern=[[1, EX], [-1, EX]], channel_multiplier=0).then_inc(low, 1)

            @block.scalar
            def _(a):
                a.wait_ge(vary, 1)
                a.activation(var[:], var[:], ACT.Sqrt).then_inc(root, 1)
                a.wait_ge(shifted, 1)
                a.activation(gate[:], gate[:], ACT.Exp).then_inc(raised, 1)

            @block.vector
            def _(v):
                ch = Chain(v, done)

                def step(i):
                    ch.inc(i)
                    ch.wait()

                def rows(ap):
                    return ap.unsqueeze(1).to_broadcast([P, NB, F])

                def each(ap, n):
                    return ap.unsqueeze(2).to_broadcast([P, NB, n])
                step(v.tensor_scalar(inv[:], acc[:, :, F:GROW], 1e-16, None, ALU.add))
                step(v.reciprocal(inv[:], inv[:]))
                step(v.tensor_tensor(y[:].rearrange("p b (h e) -> p b h e", e=EX), acc[:, :, 0:F].rearrange("p b (h e) -> p b h e", e=EX),
                                     inv[:].unsqueeze(3).to_broadcast([P, NB, GH, EX]), ALU.mult))
                v.wait_ge(loaded, 48)
                step(v.tensor_tensor(y[:], y[:], rows(par[:, 0, :]), ALU.add))
                step(v.tensor_reduce(mean[:], y[:], AX.X, ALU.add))
                step(v.tensor_scalar(mean[:], mean[:], 1.0 / F, None, ALU.mult))
                step(v.tensor_tensor(y[:], y[:], each(mean[:], F), ALU.subtract))
                step(v.tensor_tensor(y2[:], y[:], y[:], ALU.mult))
                step(v.tensor_reduce(var[:], y2[:], AX.X, ALU.add))
                v.tensor_scalar(var[:], var[:], 1.0 / F, EPS, ALU.mult, ALU.add).then_inc(vary, 1)
                v.wait_ge(root, 1)
                step(v.reciprocal(var[:], var[:]))
                step(v.tensor_tensor(y[:], y[:], each(var[:], F), ALU.mult))
                step(v.tensor_tensor(y[:], y[:], rows(par[:, 1, :]), ALU.mult))
                step(v.tensor_tensor(y[:], y[:], rows(par[:, 2, :]), ALU.add))
                step(v.tensor_reduce(sc[:], y[:].rearrange("p b (h e) -> p b e h", e=EX), AX.X, ALU.add))
                step(v.tensor_scalar(sc[:], sc[:], 1.0 / GH, None, ALU.mult))
                step(v.tensor_reduce(top[:], sc[:], AX.X, ALU.max))
                v.tensor_tensor(gate[:], sc[:], each(top[:], EX), ALU.subtract).then_inc(shifted, 1)
                other = sc[:].unsqueeze(2).to_broadcast([P, NB, EX, EX])
                own = sc[:].unsqueeze(3).to_broadcast([P, NB, EX, EX])
                step(v.tensor_tensor(less[:], other, own, ALU.is_gt))
                step(v.tensor_tensor(same[:], other, own, ALU.is_equal))
                v.wait_ge(low, 2)
                step(v.tensor_tensor(same[:], same[:], lower[:].unsqueeze(1).to_broadcast([P, NB, EX, EX]), ALU.mult))
                step(v.tensor_tensor(less[:], less[:], same[:], ALU.add))
                step(v.tensor_reduce(sc[:], less[:], AX.X, ALU.add))
                step(v.tensor_scalar(sc[:], sc[:], 1.5, None, ALU.is_lt))
                v.wait_ge(raised, 1)
                step(v.tensor_tensor(gate[:], gate[:], sc[:], ALU.mult))
                step(v.tensor_reduce(top[:], gate[:], AX.X, ALU.add))
                step(v.reciprocal(top[:], top[:]))
                step(v.tensor_tensor(gate[:], gate[:], each(top[:], EX), ALU.mult))


def combine(nc, gate, y, y_in, y_loaded, x_sb, out):
    with Region(nc, "combine") as r:
        used, added, stored = r.sem("used"), r.sem("added"), r.sem("stored")
        with nc.Block() as block:
            @block.sync
            def _(s):
                with s.Fori(1, NB // U) as it:
                    for k in range(U):
                        n = it * U + k
                        s.wait_ge(used, n + 1)
                        load_y(s, y, y_in, y_loaded, n, k)

            @block.scalar
            def _(a):
                def store(n):
                    a.wait_ge(used, n + 1 + U)
                    a.dma_start(out[bass.ds(n * P, P), :], x_sb[:, n, :]).then_inc(stored, 16)
                with a.Fori(0, FULL // U) as it:
                    for k in range(U):
                        store(it * U + k)
                for n in range(FULL // U * U, FULL):
                    store(n)
                a.wait_ge(used, FULL + 1 + U)
                a.dma_start(out[FULL * P:N, :], x_sb[0:REST, FULL, :]).then_inc(stored, 16)
                a.wait_ge(stored, 16 * (FULL + 1))

            @block.vector
            def _(v):
                v.sem_inc(used, U)
                with v.Fori(0, NB // U) as it:
                    for k in range(U):
                        n = it * U + k
                        v.wait_ge(y_loaded[k], it * 16 + 16)
                        for e in range(EX):
                            if e:
                                v.wait_ge(added, n * (EX - 1) + e)
                            i = v.scalar_tensor_tensor(out=x_sb[:, n, :], in0=y_in[k][:, e, :], scalar=gate[:, n, e:e + 1],
                                                       in1=x_sb[:, n, :], op0=ALU.mult, op1=ALU.add)
                            i.then_inc(added if e + 1 < EX else used, 1)


def program(nc, x, att_key_tile, att_idx_tile, att_key_flat, Wq, bq, Wk, bk, Wv, bv, Wo, bo,
            gat_key_tile, gat_idx_tile, gat_key_flat, W_gat, att_src, att_dst, b_gat, ln_gamma, ln_beta, W1, b1, W2, b2, out):
    def dram(name, shape, dt=F32):
        return nc.dram_tensor(name, shape, dt).ap()

    def ordered(r, g, key_tile, idx_tile, key_flat):
        n = g.name
        idx, lo = r.sb(n + "_idx", [P, g.slots], I32), r.sb(n + "_lo", [P, g.slots])
        block, first = r.sb(n + "_block", [1, g.items], I32), r.sb(n + "_first", [KEYS_HI, 1])
        rows, key_line, lo_line = dram(n + "_rows", (g.pos, 4)), dram(n + "_key_line", (g.pos,)), dram(n + "_lo_line", (g.pos,))
        sort_edges(nc, c, g, key_tile, idx_tile, key_flat, rows, first)
        unpack(nc, c, g, rows, first, key_line, lo_line, idx, lo, block)
        return idx, lo, block, key_line, lo_line

    with Region(nc, "top") as top:
        c = {"ident": top.sb("ident", [P, P]), "iota": top.sb("iota", [P, P]), "col": top.sb("col", [P, 1])}
        x_sb, x_loaded = top.sb("x_sb", [P, NB, D]), top.sem("x_loaded")
        constants(nc, c, x, x_sb, x_loaded)
        with Region(nc, "att") as r0:
            idx, lo, block, key_line, lo_line = ordered(r0, ATT, att_key_tile, att_idx_tile, att_key_flat)
            scores, probs = dram("att_scores", (ATT.slots, HEADS, P)), dram("att_probs", (ATT.slots, HEADS, P))
            k_rows, v_rows = dram("k_rows", (NPAD, D)), dram("v_rows", (NPAD, D))
            with Region(nc, "q") as r:
                q_sb = r.sb("q_sb", [P, NB, D])
                with Region(nc, "centred") as r2:
                    xc, rstd = r2.sb("xc", [P, NB, D]), r2.sb("rstd", [P, NB])
                    normalise(nc, "norm0", x_sb, xc, rstd, x_loaded)
                    project(nc, c, xc, rstd, {"Wq": Wq, "bq": bq, "Wk": Wk, "bk": bk, "Wv": Wv, "bv": bv}, q_sb, (k_rows, v_rows))
                attention_scores(nc, c, ATT, idx, lo_line, block, q_sb, k_rows, scores)
            segment_softmax(nc, c, ATT, HEADS, scores, key_line, probs)
            with Region(nc, "sums") as r:
                acc = r.sb("acc", [P, NB, D + HEADS])
                attention_sum(nc, c, ATT, idx, lo, block, v_rows, probs, acc)
                attention_out(nc, c, acc, Wo, bo, x_sb)
        with Region(nc, "gat") as r:
            idx, lo, block, key_line, lo_line = ordered(r, GAT, gat_key_tile, gat_idx_tile, gat_key_flat)
            scores, probs = dram("gat_scores", (GAT.slots, GH, P)), dram("gat_probs", (GAT.slots, GH, P))
            table, kept_rows = dram("gat_table", (NPAD, GROW)), dram("gat_kept", (GAT.items // GI * P, GT * GROW))
            xT_all = r.sb("xT_all", [P, 2, NPAD])
            a_dst, gate = r.sb("a_dst", [P, NB, GH]), r.sb("gate", [P, NB, EX])
            acc = r.sb("acc", [P, NB, GROW])
            with Region(nc, "centred2") as r2:
                xc, rstd = r2.sb("xc", [P, NB, D]), r2.sb("rstd", [P, NB])
                normalise(nc, "norm1", x_sb, xc, rstd)
                gat_rows(nc, c, xc, rstd, W_gat, att_src, att_dst, xT_all, table, a_dst)
            y = dram("expert_out", (NPAD, EX * D))
            gat_scores_and_experts(nc, c, GAT, idx, lo_line, block, table, a_dst, kept_rows, scores, xT_all, W1, b1, W2, b2, y)
            segment_softmax(nc, c, GAT, GH, scores, key_line, probs)
            gat_sum(nc, c, GAT, lo, block, kept_rows, probs, acc)
            y_in = [r.sb(f"y_in{k}", [P, EX, D]) for k in range(U)]
            y_loaded = [r.sem(f"y_loaded{k}") for k in range(U)]
            route(nc, c, acc, b_gat, ln_gamma, ln_beta, gate, y, y_in, y_loaded)
            combine(nc, gate, y, y_in, y_loaded, x_sb, out)


def kernel(x, src, dst, L0_gnn_Wq, L0_gnn_bq, L0_gnn_Wk, L0_gnn_bk, L0_gnn_Wv, L0_gnn_bv, L0_gnn_Wo, L0_gnn_bo,
           L0_ffn_W_gat, L0_ffn_att_src, L0_ffn_att_dst, L0_ffn_b_gat, L0_ffn_ln_gamma, L0_ffn_ln_beta,
           L0_ffn_W1, L0_ffn_b1, L0_ffn_W2, L0_ffn_b2, L0_ffn_edge_index):
    import numpy as np
    import concourse.bacc as bacc
    from concourse.bass_utils import run_bass_kernel_spmd

    def lists(g, key, idx):
        flat = np.full((2, g.tiles * P), 0, np.int32)
        flat[0, :] = PAD_KEY
        flat[0, 0:key.size] = key
        flat[1, 0:idx.size] = idx
        by_tile = [np.ascontiguousarray(a.reshape(g.tiles, P).T) for a in flat]
        return by_tile[0], by_tile[1], np.ascontiguousarray(flat[0])

    loops = np.arange(BLOCKS * P, dtype=np.int32)
    edge = np.asarray(L0_ffn_edge_index)
    att = lists(ATT, np.asarray(src), np.asarray(dst))
    gat = lists(GAT, np.concatenate([edge[1], loops]), np.concatenate([edge[0], loops]))
    given = [x, *att, L0_gnn_Wq, L0_gnn_bq, L0_gnn_Wk, L0_gnn_bk, L0_gnn_Wv, L0_gnn_bv, L0_gnn_Wo, L0_gnn_bo, *gat,
             L0_ffn_W_gat, L0_ffn_att_src, L0_ffn_att_dst, L0_ffn_b_gat, L0_ffn_ln_gamma, L0_ffn_ln_beta,
             L0_ffn_W1, L0_ffn_b1, L0_ffn_W2, L0_ffn_b2]
    nc = bacc.Bacc("TRN2", target_bir_lowering=False, num_devices=1)
    arrays, args = {}, []
    for i, a in enumerate(given):
        a = np.ascontiguousarray(a)
        arrays[f"in_{i}"] = a
        args.append(nc.dram_tensor(f"in_{i}", a.shape, mybir.dt.from_np(a.dtype), kind="ExternalInput").ap())
    out = nc.dram_tensor("out", (N, D), F32, kind="ExternalOutput").ap()
    program(nc, *args, out)
    got = run_bass_kernel_spmd(nc, [arrays], core_ids=[0])
    return got.results[0]["out"]
```
